# Optimizing a Trainium2 kernel written in Bass

```python
import numpy as np
import jax
import jax.numpy as jnp

def _softmax(x, axis=-1):
    return jax.nn.softmax(x, axis=axis)

def _gelu(x):
    return jax.nn.gelu(x, approximate=True)

def _silu(x):
    return jax.nn.silu(x)

def _sigmoid(x):
    return jax.nn.sigmoid(x)

def _layernorm(x, axis=-1, eps=1e-05):
    m = jnp.mean(x, axis=axis, keepdims=True)
    v = jnp.var(x, axis=axis, keepdims=True)
    return (x - m) / jnp.sqrt(v + eps)

def _scatter_add(tgt, idx, src, axis=0):
    return tgt.at[idx].add(src)

def _segment_sum(src, seg, n):
    return jax.ops.segment_sum(src, seg, n)
kernel_name = 'mk_dlrm_tower_d1_rec_r8_67a9bd'

def setup_inputs(seed: int=0):
    np.random.seed(seed)
    _w = jnp.asarray

    def _rec_inputs():
        import jax
        import jax.numpy as jnp
        _tk = jax.random.key(seed)
        dense_ctx = jax.random.normal(jax.random.fold_in(_tk, 190), (512, 16), jnp.float32)
        ids = jnp.stack([jax.random.randint(jax.random.fold_in(_tk, 200 + f), (512,), 0, v, jnp.int32) for f, v in enumerate([1250, 1000, 12500, 12500, 125000, 1000, 125000, 12500, 125000, 1000, 1250, 12500, 12500, 1000, 1000, 125000, 125000, 1250, 125000, 1000, 12500, 1250, 12500, 12500, 1250, 1000])], axis=1)
        tbl_0 = 0.05 * jax.random.normal(jax.random.fold_in(_tk, 500 + 0), (1250, 32), jnp.float32)
        tbl_1 = 0.05 * jax.random.normal(jax.random.fold_in(_tk, 500 + 1), (1000, 32), jnp.float32)
        tbl_2 = 0.05 * jax.random.normal(jax.random.fold_in(_tk, 500 + 2), (12500, 32), jnp.float32)
        tbl_3 = 0.05 * jax.random.normal(jax.random.fold_in(_tk, 500 + 3), (12500, 32), jnp.float32)
        tbl_4 = 0.05 * jax.random.normal(jax.random.fold_in(_tk, 500 + 4), (125000, 32), jnp.float32)
        tbl_5 = 0.05 * jax.random.normal(jax.random.fold_in(_tk, 500 + 5), (1000, 32), jnp.float32)
        tbl_6 = 0.05 * jax.random.normal(jax.random.fold_in(_tk, 500 + 6), (125000, 32), jnp.float32)
        tbl_7 = 0.05 * jax.random.normal(jax.random.fold_in(_tk, 500 + 7), (12500, 32), jnp.float32)
        tbl_8 = 0.05 * jax.random.normal(jax.random.fold_in(_tk, 500 + 8), (125000, 32), jnp.float32)
        tbl_9 = 0.05 * jax.random.normal(jax.random.fold_in(_tk, 500 + 9), (1000, 32), jnp.float32)
        tbl_10 = 0.05 * jax.random.normal(jax.random.fold_in(_tk, 500 + 10), (1250, 32), jnp.float32)
        tbl_11 = 0.05 * jax.random.normal(jax.random.fold_in(_tk, 500 + 11), (12500, 32), jnp.float32)
        tbl_12 = 0.05 * jax.random.normal(jax.random.fold_in(_tk, 500 + 12), (12500, 32), jnp.float32)
        tbl_13 = 0.05 * jax.random.normal(jax.random.fold_in(_tk, 500 + 13), (1000, 32), jnp.float32)
        tbl_14 = 0.05 * jax.random.normal(jax.random.fold_in(_tk, 500 + 14), (1000, 32), jnp.float32)
        tbl_15 = 0.05 * jax.random.normal(jax.random.fold_in(_tk, 500 + 15), (125000, 32), jnp.float32)
        tbl_16 = 0.05 * jax.random.normal(jax.random.fold_in(_tk, 500 + 16), (125000, 32), jnp.float32)
        tbl_17 = 0.05 * jax.random.normal(jax.random.fold_in(_tk, 500 + 17), (1250, 32), jnp.float32)
        tbl_18 = 0.05 * jax.random.normal(jax.random.fold_in(_tk, 500 + 18), (125000, 32), jnp.float32)
        tbl_19 = 0.05 * jax.random.normal(jax.random.fold_in(_tk, 500 + 19), (1000, 32), jnp.float32)
        tbl_20 = 0.05 * jax.random.normal(jax.random.fold_in(_tk, 500 + 20), (12500, 32), jnp.float32)
        tbl_21 = 0.05 * jax.random.normal(jax.random.fold_in(_tk, 500 + 21), (1250, 32), jnp.float32)
        tbl_22 = 0.05 * jax.random.normal(jax.random.fold_in(_tk, 500 + 22), (12500, 32), jnp.float32)
        tbl_23 = 0.05 * jax.random.normal(jax.random.fold_in(_tk, 500 + 23), (12500, 32), jnp.float32)
        tbl_24 = 0.05 * jax.random.normal(jax.random.fold_in(_tk, 500 + 24), (1250, 32), jnp.float32)
        tbl_25 = 0.05 * jax.random.normal(jax.random.fold_in(_tk, 500 + 25), (1000, 32), jnp.float32)
        _rk = jax.random.fold_in(_tk, 7)
        W_top1 = 0.0606339 * jax.random.normal(jax.random.fold_in(_tk, 801), (272, 512), jnp.float32)
        W_top2 = 0.0441942 * jax.random.normal(jax.random.fold_in(_tk, 802), (512, 256), jnp.float32)
        W_top3 = 0.0625 * jax.random.normal(jax.random.fold_in(_tk, 803), (256, 1), jnp.float32)
        b_top1 = jnp.zeros((512,), jnp.float32)
        b_top2 = jnp.zeros((256,), jnp.float32)
        return (dense_ctx, ids, tbl_0, tbl_1, tbl_2, tbl_3, tbl_4, tbl_5, tbl_6, tbl_7, tbl_8, tbl_9, tbl_10, tbl_11, tbl_12, tbl_13, tbl_14, tbl_15, tbl_16, tbl_17, tbl_18, tbl_19, tbl_20, tbl_21, tbl_22, tbl_23, tbl_24, tbl_25, W_top1, b_top1, W_top2, b_top2, W_top3)
    dense_ctx, ids, tbl_0, tbl_1, tbl_2, tbl_3, tbl_4, tbl_5, tbl_6, tbl_7, tbl_8, tbl_9, tbl_10, tbl_11, tbl_12, tbl_13, tbl_14, tbl_15, tbl_16, tbl_17, tbl_18, tbl_19, tbl_20, tbl_21, tbl_22, tbl_23, tbl_24, tbl_25, W_top1, b_top1, W_top2, b_top2, W_top3 = _rec_inputs()

    def _L0_rec_setup():
        import jax, jax.numpy as jnp
        import numpy as np
        M_FIELDS = 26
        H1 = 128
        H2 = 128
        BATCH = 256
        EMB_K = 32

        def _cin_layer(x_prev, x0, W, b):
            return jnp.einsum('bik,bjk,hij->bhk', x_prev, x0, W) + b[None, :, None]
        key = jax.random.key(seed)
        k0, k1, k2, k3, k4 = jax.random.split(key, 5)
        inputs = jax.random.normal(k0, (BATCH, M_FIELDS, EMB_K), dtype=jnp.float32)
        W1 = jax.random.normal(k1, (H1, M_FIELDS, M_FIELDS), dtype=jnp.float32) * 0.05
        b1 = jax.random.normal(k2, (H1,), dtype=jnp.float32) * 0.05
        W2 = jax.random.normal(k3, (H2, H1, M_FIELDS), dtype=jnp.float32) * 0.05
        b2 = jax.random.normal(k4, (H2,), dtype=jnp.float32) * 0.05
        return {'inputs': inputs, 'W1': W1, 'b1': b1, 'W2': W2, 'b2': b2}
    _L0_rec_all = _L0_rec_setup()
    _L0_rec_in = {k: v for k, v in _L0_rec_all.items() if k in ('W1', 'b1', 'W2', 'b2')}
    del _L0_rec_all
    return {'dense_ctx': dense_ctx, 'ids': ids, 'tbl_0': tbl_0, 'tbl_1': tbl_1, 'tbl_2': tbl_2, 'tbl_3': tbl_3, 'tbl_4': tbl_4, 'tbl_5': tbl_5, 'tbl_6': tbl_6, 'tbl_7': tbl_7, 'tbl_8': tbl_8, 'tbl_9': tbl_9, 'tbl_10': tbl_10, 'tbl_11': tbl_11, 'tbl_12': tbl_12, 'tbl_13': tbl_13, 'tbl_14': tbl_14, 'tbl_15': tbl_15, 'tbl_16': tbl_16, 'tbl_17': tbl_17, 'tbl_18': tbl_18, 'tbl_19': tbl_19, 'tbl_20': tbl_20, 'tbl_21': tbl_21, 'tbl_22': tbl_22, 'tbl_23': tbl_23, 'tbl_24': tbl_24, 'tbl_25': tbl_25, 'W_top1': W_top1, 'b_top1': b_top1, 'W_top2': W_top2, 'b_top2': b_top2, 'W_top3': W_top3, 'L0_rec_W1': _L0_rec_in['W1'], 'L0_rec_b1': _L0_rec_in['b1'], 'L0_rec_W2': _L0_rec_in['W2'], 'L0_rec_b2': _L0_rec_in['b2']}

def reference(dense_ctx, ids, tbl_0, tbl_1, tbl_2, tbl_3, tbl_4, tbl_5, tbl_6, tbl_7, tbl_8, tbl_9, tbl_10, tbl_11, tbl_12, tbl_13, tbl_14, tbl_15, tbl_16, tbl_17, tbl_18, tbl_19, tbl_20, tbl_21, tbl_22, tbl_23, tbl_24, tbl_25, W_top1, b_top1, W_top2, b_top2, W_top3, L0_rec_W1, L0_rec_b1, L0_rec_W2, L0_rec_b2):
    import jax
    import jax.numpy as jnp

    def _L0_rec_ref(inputs, W1, b1, W2, b2):
        import jax, jax.numpy as jnp
        import numpy as np
        M_FIELDS = 26
        H1 = 128
        H2 = 128
        BATCH = 256
        EMB_K = 32

        def _cin_layer(x_prev, x0, W, b):
            return jnp.einsum('bik,bjk,hij->bhk', x_prev, x0, W) + b[None, :, None]
        x1 = _cin_layer(inputs, inputs, W1, b1)
        x2 = _cin_layer(x1, inputs, W2, b2)
        res = jnp.concatenate([x1, x2], axis=1)
        return jnp.sum(res, axis=-1)
    e = jnp.stack([tbl_0[ids[:, 0]], tbl_1[ids[:, 1]], tbl_2[ids[:, 2]], tbl_3[ids[:, 3]], tbl_4[ids[:, 4]], tbl_5[ids[:, 5]], tbl_6[ids[:, 6]], tbl_7[ids[:, 7]], tbl_8[ids[:, 8]], tbl_9[ids[:, 9]], tbl_10[ids[:, 10]], tbl_11[ids[:, 11]], tbl_12[ids[:, 12]], tbl_13[ids[:, 13]], tbl_14[ids[:, 14]], tbl_15[ids[:, 15]], tbl_16[ids[:, 16]], tbl_17[ids[:, 17]], tbl_18[ids[:, 18]], tbl_19[ids[:, 19]], tbl_20[ids[:, 20]], tbl_21[ids[:, 21]], tbl_22[ids[:, 22]], tbl_23[ids[:, 23]], tbl_24[ids[:, 24]], tbl_25[ids[:, 25]]], axis=1)
    z = _L0_rec_ref(e, L0_rec_W1, L0_rec_b1, L0_rec_W2, L0_rec_b2)
    z = z.reshape(z.shape[0], -1)
    h = jnp.concatenate([z, dense_ctx], axis=1)
    h = jnp.maximum(h @ W_top1 + b_top1, 0.0)
    h = jnp.maximum(h @ W_top2 + b_top2, 0.0)
    y = h @ W_top3
    return y

_drawn_inputs = setup_inputs


def setup_inputs(seed=0):
    import zlib

    import numpy as np

    out = dict(_drawn_inputs(seed))
    spreads = {'b_top1': (0.0, 2.0), 'b_top2': (0.0, 0.8)}
    factors = {'tbl_0': 8.0,
     'tbl_1': 8.0,
     'tbl_2': 8.0,
     'tbl_3': 8.0,
     'tbl_4': 8.0,
     'tbl_5': 8.0,
     'tbl_6': 8.0,
     'tbl_7': 8.0,
     'tbl_8': 8.0,
     'tbl_9': 8.0,
     'tbl_10': 8.0,
     'tbl_11': 8.0,
     'tbl_12': 8.0,
     'tbl_13': 8.0,
     'tbl_14': 8.0,
     'tbl_15': 8.0,
     'tbl_16': 8.0,
     'tbl_17': 8.0,
     'tbl_18': 8.0,
     'tbl_19': 8.0,
     'tbl_20': 8.0,
     'tbl_21': 7.843,
     'tbl_22': 8.0,
     'tbl_23': 8.0,
     'tbl_24': 8.0,
     'tbl_25': 8.0,
     'L0_rec_W1': 7.989,
     'L0_rec_W2': 4.2,
     'dense_ctx': 5.94}
    for name, (base, spread) in spreads.items():
        noise = np.random.default_rng([zlib.crc32(name.encode()), seed]).standard_normal(out[name].shape)
        drawn = base * np.exp(spread * noise) if base else spread * noise
        out[name] = jnp.asarray(drawn.astype(out[name].dtype))
    for name, factor in factors.items():
        out[name] = (out[name] * factor).astype(out[name].dtype)
    return out
```

```python
import concourse.bass as bass
from concourse import mybir
from contextlib import ExitStack


def dlrm_cin_tower(nc, x, out):
    fp32 = mybir.dt.float32
    i32 = mybir.dt.int32
    ALU = mybir.AluOpType
    ACT = mybir.ActivationFunctionType

    P = 128
    B, F = x["ids"].shape
    K = x["tbl_0"].shape[1]
    H = x["L0_rec_W1"].shape[0]
    DC = x["dense_ctx"].shape[1]
    O1 = x["W_top2"].shape[0]
    O2 = x["W_top3"].shape[0]
    T = B // P
    Q = P // K
    NG = P // Q
    HF = F // 2
    OFF = HF * (HF - 1) // 2
    NP = HF + OFF
    ONE = NP
    EF = NP + 1
    MA = EF + F
    PB = MA
    NS = MA + NP
    DB = NP + 1
    DX = DB + NP
    ND = DX + HF * HF
    GP = 4
    NB = NG // GP
    RING = 4
    JG = -(-F // 4)
    W_AT_ONCE = 4
    C1, C2 = O1 // P, O2 // P

    def off(y):
        return HF + y * (y - 1) // 2

    ctx = ExitStack()
    with ctx:
        def sb(name, shape, dt=fp32):
            return ctx.enter_context(nc.sbuf_tensor(name, shape, dt))

        def sem(name):
            return ctx.enter_context(nc.semaphore(name))

        idx = sb("idx", [P, T, F], i32)
        E = sb("E", [P, T, F, K])
        late = sb("late", [P, NS * NG + 2 * JG * P + 2 * (2 + C1 + C2) * P])
        taken = [0]

        def part(n):
            taken[0] += n * P
            return late[:, taken[0] - n * P:taken[0]].rearrange("p (n b) -> p n b", b=P)

        D = late[:, 0:F * ND].rearrange("p (j n) -> p j n", n=ND)
        PT1 = late[:, 0:NS * NG].rearrange("p (s g) -> p s g", g=NG)
        taken[0] = NS * NG
        PT = [sb("PT0", [P, NS, NG]), PT1]
        BD = [sb(f"BD{i}", [P, NG, Q * F]) for i in range(2)]
        CA = [sb(f"CA{i}", [P, F, P]) for i in range(2)]
        CB = [sb(f"CB{i}", [P, F, P]) for i in range(2)]
        G4 = [part(JG) for i in range(2)]
        w1 = sb("w1", [H, F, F])
        w2 = CA[1][:, :, :].rearrange("p a b -> p (a b)").rearrange("p (m j) -> p m j", j=F)
        w2T = CB[1]
        S = sb("S", [H, ND])
        VA = sb("VA", [NP + 1, F, H])
        VB = sb("VB", [NP, F, H])
        W1G = sb("W1G", [4 * F, JG, H])
        ident = sb("ident", [P, P])
        wt1 = sb("wt1", [P, 2, O1])
        wt1d = sb("wt1d", [DC, O1])
        wt2 = sb("wt2", [P, C1, O2])
        wt3 = sb("wt3", [P, C2])
        bt1 = sb("bt1", [P, C1])
        bt2 = sb("bt2", [P, C2])
        b12 = sb("b12", [P, 2])
        b12k = sb("b12k", [P, 2])
        dn = sb("dn", [P, T, DC])
        dT = sb("dT", [DC, T, P])
        z = [part(2) for i in range(2)]
        h1 = [part(C1) for i in range(2)]
        h2 = [part(C2) for i in range(2)]
        y = sb("y", [1, T, P])
        bank = [ctx.enter_context(nc.psum_tensor(f"bank{i}", [P, 512], fp32)) for i in range(8)]

        ids_in, w1_in, w2_in, b12_in, b1_in = sem("ids_in"), sem("w1_in"), sem("w2_in"), sem("b12_in"), sem("b1_in")
        top_in, dn_in = sem("top_in"), sem("dn_in")
        gathered = [sem(f"gathered{t}") for t in range(T)]
        ident_zero, ident_ok = sem("ident_zero"), sem("ident_ok")
        s_ready = sem("s_ready")
        bd_zero = sem("bd_zero")
        prep_ps = sem("prep_ps")
        prep_sb = sem("prep_sb")
        sym_ok = sem("sym_ok")
        chain = sem("chain")
        e_ok = sem("e_ok")
        bd_ok = sem("bd_ok")
        pair_ok = sem("pair_ok")
        c_ps = sem("c_ps")
        c_sb = sem("c_sb")
        g_in = [sem(f"g_in{i}") for i in range(2)]
        f_done = sem("f_done")
        z_ok = sem("z_ok")
        l1_ps, l1_ok = sem("l1_ps"), sem("l1_ok")
        l2_ps, l2_ok = sem("l2_ps"), sem("l2_ok")
        l3_ps, y_ok, y_out = sem("l3_ps"), sem("y_ok"), sem("y_out")

        prep = ([("w2T", j) for j in range(0, F, W_AT_ONCE)] + [("d", 0)] + [("D", j) for j in range(F)]
                + [("w1", s) for s in range(0, JG, W_AT_ONCE)])
        prep_late = [("VA", j) for j in range(0, F, W_AT_ONCE)] + [("VB", j) for j in range(0, F, W_AT_ONCE)]
        N_W2T = -(-F // W_AT_ONCE)
        UNITS = 2 * NB

        def prep_bank(n):
            return bank[4 + n % RING]

        def g_rows(s):
            return min(4, F - 4 * s)

        block = ctx.enter_context(nc.Block())

        @block.sync
        def _(sp):
            sp.dma_start(idx[:, :, :], x["ids"].rearrange("(t p) f -> p t f", p=P)).then_inc(ids_in, 16)
            sp.dma_start(w2[:, :, :], x["L0_rec_W2"][:, :, :]).then_inc(w2_in, 16)
            sp.dma_start(w1[:, :, :], x["L0_rec_W1"][:, :, :]).then_inc(w1_in, 16)
            b1c = x["L0_rec_b1"].rearrange("(h o) -> h o", o=1)
            b2c = x["L0_rec_b2"].rearrange("(h o) -> h o", o=1)
            sp.dma_start(S[:, NP:NP + 1], b1c).then_inc(b1_in, 16)
            sp.dma_start(b12[:, 0:1], b1c).then_inc(b12_in, 16)
            sp.dma_start(b12[:, 1:2], b2c).then_inc(b12_in, 16)
            sp.dma_start(dn[:, :, :], x["dense_ctx"].rearrange("(t p) c -> p t c", p=P)).then_inc(dn_in, 16)
            sp.dma_start(wt1[:, :, :], x["W_top1"][0:2 * P, :].rearrange("(c p) o -> p c o", p=P)).then_inc(top_in, 16)
            sp.dma_start(wt1d[:, :], x["W_top1"][2 * P:, :]).then_inc(top_in, 16)
            sp.dma_start(wt2[:, :, :], x["W_top2"].rearrange("(p c) o -> p c o", c=C1)).then_inc(top_in, 16)
            sp.dma_start(wt3[:, :], x["W_top3"].rearrange("(p c) o -> p (c o)", c=C2)).then_inc(top_in, 16)
            sp.dma_start(bt1[:, :], x["b_top1"].rearrange("(p c) -> p c", c=C1)).then_inc(top_in, 16)
            sp.dma_start(bt2[:, :], x["b_top2"].rearrange("(p c) -> p c", c=C2)).then_inc(top_in, 16)
            for t in range(T):
                sp.wait_ge(c_sb, UNITS * (t + 1))
                if t == 0:
                    sp.wait_ge(prep_ps, len(prep) + len(prep_late))
                if t >= 2:
                    sp.wait_ge(f_done, t - 1)
                for q in range(4):
                    n = len(range(q, F, 4))
                    sp.dma_start(G4[t % 2][q * F:(q + 1) * F, 0:n, :],
                                 CA[t % 2][EF:EF + F, q::4, :]).then_inc(g_in[t % 2], 16)
            sp.wait_ge(y_ok, T)
            sp.dma_start(out.rearrange("b o -> o b"), y[:, :, :].rearrange("o t p -> o (t p)")).then_inc(y_out, 16)
            sp.wait_ge(y_out, 16)

        @block.gpsimd
        def _(pool):
            nc.gpsimd.memset(ident[:, :], 0.0).then_inc(ident_zero, 1)
            pool.wait_ge(ident_zero, 1)
            nc.gpsimd.affine_select(out=ident[:, :], in_=ident[:, :], compare_op=ALU.not_equal, fill=1.0, base=0,
                                    pattern=[[-1, P]], channel_multiplier=1).then_inc(ident_ok, 1)
            pool.wait_ge(ids_in, 16)
            for t in range(T):
                for f in range(F):
                    pool.indirect_dma_start(
                        out=E[:, t, f, :], out_offset=None, in_=x[f"tbl_{f}"][:, :],
                        in_offset=bass.IndirectOffsetOnAxis(ap=idx[:, t, f:f + 1], axis=0)).then_inc(gathered[t], 16)

        @block.vector
        def _(dve):
            links = [0]

            def link(ins):
                links[0] += 1
                ins.then_inc(chain, 1)
                dve.wait_ge(chain, links[0])

            for i in range(2):
                last = nc.vector.memset(BD[i][:, :, :], 0.0)
            last.then_inc(bd_zero, 1)
            dve.wait_ge(w1_in, 16)
            wf = w1[:, :, :].rearrange("p i j -> p (i j)")
            for half, base in ((0, 0), (HF, DB)):
                d0 = half * (F + 1)
                nc.vector.tensor_copy(S[:, base:base + HF], wf[:, d0:d0 + (HF - 1) * (F + 1) + 1:F + 1])
                for n in range(1, HF):
                    nc.vector.tensor_tensor(S[:, base + off(n):base + off(n) + n], w1[:, half:half + n, half + n],
                                            w1[:, half + n, half:half + n], ALU.add)
            nc.vector.tensor_tensor(S[:, DX:].rearrange("p (a b) -> p a b", b=HF), w1[:, 0:HF, HF:],
                                    w1[:, HF:, 0:HF].rearrange("p b a -> p a b"), ALU.add).then_inc(s_ready, 1)
            dve.wait_ge(b12_in, 32)
            nc.vector.tensor_scalar(b12k[:, :], b12[:, :], float(K), None, ALU.mult)

            def pairs(t):
                buf = PT[t % 2]
                dve.wait_ge(gathered[t], 16 * F)
                if t == 1:
                    dve.wait_ge(prep_ps, len(prep) + len(prep_late))
                if t >= 2:
                    dve.wait_ge(c_ps, UNITS * (t - 1))
                if t < 2:
                    nc.vector.memset(buf[:, ONE, :], 1.0)
                nc.vector.transpose(buf[:, EF:EF + F, :].rearrange("p f g -> p (f g)"),
                                    E[:, t, :, :].rearrange("p f k -> p (f k)")).then_inc(e_ok, 1)
                dve.wait_ge(e_ok, t + 1)
                for half, base in ((EF, 0), (EF + HF, PB)):
                    e = buf[:, half:half + HF, :]
                    last = nc.vector.tensor_tensor(buf[:, base:base + HF, :], e, e, ALU.mult)
                    for n in range(1, HF):
                        last = nc.vector.tensor_tensor(buf[:, base + off(n):base + off(n) + n, :], e[:, 0:n, :],
                                                       e[:, n:n + 1, :].to_broadcast([P, n, NG]), ALU.mult)
                last.then_inc(pair_ok, 1)

            def symmetrize():
                dve.wait_ge(prep_sb, len(prep))
                X = D[:, :, DX:].rearrange("p j (a b) -> p j a b", b=HF)
                Df = D[:, :, :].rearrange("p j n -> p (j n)")
                for n in range(HF):
                    link(nc.vector.tensor_tensor(D[:, HF:, n], D[:, HF:, n], X[:, n, n, :], ALU.add))
                    link(nc.vector.tensor_tensor(D[:, 0:HF, DB + n], D[:, 0:HF, DB + n], X[:, HF + n, :, n], ALU.add))
                for n in range(1, HF):
                    a = D[:, HF:, off(n):off(n) + n]
                    b = D[:, 0:HF, DB + off(n):DB + off(n) + n]
                    link(nc.vector.tensor_tensor(a, a, X[:, 0:n, n, :].rearrange("p x b -> p b x"), ALU.add))
                    link(nc.vector.tensor_tensor(b, b, X[:, HF:HF + n, :, n].rearrange("p x a -> p a x"), ALU.add))
                    link(nc.vector.tensor_tensor(a, a, X[:, n, 0:n, :].rearrange("p x b -> p b x"), ALU.add))
                    link(nc.vector.tensor_tensor(b, b, X[:, HF + n, :, 0:n], ALU.add))
                nc.vector.tensor_copy(y[:, 0, 0:1], D[0:1, 0, 0:1]).then_inc(sym_ok, 1)

            def z_out(t):
                dve.wait_ge(f_done, t + 1)
                if t >= 2:
                    dve.wait_ge(l1_ps, t - 1)
                zb = bank[4 + t % 2]
                nc.vector.tensor_scalar(z[t % 2][:, 0, :], zb[:, P:2 * P], b12k[:, 0:1], None, ALU.add)
                nc.vector.tensor_scalar(z[t % 2][:, 1, :], zb[:, 0:P], b12k[:, 1:2], None, ALU.add).then_inc(z_ok, 1)

            def relu(dst, src, bias, n):
                for c in range(n):
                    last = nc.vector.tensor_scalar(dst[:, c, :], src[:, c * P:(c + 1) * P], bias[:, c:c + 1], 0.0,
                                                   ALU.add, ALU.max)
                return last

            def l1_out(t):
                dve.wait_ge(l1_ps, t + 1)
                if t >= 2:
                    dve.wait_ge(l2_ps, t - 1)
                relu(h1[t % 2], bank[6], bt1, C1).then_inc(l1_ok, 1)

            def l2_out(t):
                dve.wait_ge(l2_ps, t + 1)
                if t >= 2:
                    dve.wait_ge(l3_ps, t - 1)
                relu(h2[t % 2], bank[7], bt2, C2).then_inc(l2_ok, 1)

            def l3_out(t):
                dve.wait_ge(l3_ps, t + 1)
                nc.vector.tensor_copy(y[:, t, :], bank[7][0:1, 2 * P:3 * P]).then_inc(y_ok, 1)

            dve.wait_ge(top_in, 16 * 6)
            pairs(0)
            symmetrize()
            pairs(1)
            for t in range(2, T):
                z_out(t - 2)
                pairs(t)
                l1_out(t - 2)
                l2_out(t - 2)
                l3_out(t - 2)
            for t in range(T - 2, T):
                z_out(t)
                l1_out(t)
                l2_out(t)
                l3_out(t)

        @block.scalar
        def _(act):
            def empty(plan, first):
                for n, (kind, j) in enumerate(plan, first):
                    act.wait_ge(prep_ps, n + 1)
                    src = prep_bank(n)
                    if kind == "d":
                        dst, src = dT[:, :, :], src[0:DC, 0:T * P].rearrange("c (t p) -> c t p", p=P)
                    elif kind == "D":
                        dst, src = D[:, j, :], src[:, 0:ND]
                    else:
                        full = {"w2T": w2T, "w1": W1G, "VA": VA, "VB": VB}[kind]
                        m = min(W_AT_ONCE, full.shape[1] - j)
                        dst = full[:, j:j + m, :]
                        src = src[0:full.shape[0], 0:m * P].rearrange("p (j h) -> p j h", h=H)
                    nc.scalar.copy(dst, src).then_inc(prep_sb, 1)

            def block_diagonal(t):
                act.wait_ge(e_ok, t + 1)
                if t == 0:
                    act.wait_ge(bd_zero, 1)
                if t >= 2:
                    act.wait_ge(c_ps, UNITS * (t - 1))
                for q in range(Q):
                    rows = slice(q * K, (q + 1) * K)
                    last = nc.scalar.copy(BD[t % 2][rows, :, q * F:(q + 1) * F],
                                          PT[t % 2][rows, EF:EF + F, :].rearrange("p f g -> p g f"))
                last.then_inc(bd_ok, 1)

            def moments(t):
                if t >= 2:
                    act.wait_ge(f_done, t - 1)
                    act.wait_ge(g_in[t % 2], 64 * (t // 2))
                for n in range(UNITS):
                    u = UNITS * t + n
                    act.wait_ge(c_ps, u + 1)
                    C, rows = ((CA, MA), (CB, NP))[n % 2]
                    g0 = (n // 2) * GP
                    dst = C[t % 2][0:rows, :, :].rearrange("s j (q g) -> s g q j", q=Q)[:, g0:g0 + GP, :, :]
                    src = bank[u % RING][0:rows, 0:GP * Q * F].rearrange("s (g q j) -> s g q j", g=GP, q=Q)
                    for g in range(GP):
                        last = nc.scalar.copy(dst[:, g, :, :], src[:, g, :, :])
                    last.then_inc(c_sb, 1)

            empty(prep, 0)
            for t in range(T):
                block_diagonal(t)
                moments(t)
                if t == 0:
                    empty(prep_late, len(prep))

        @block.tensor
        def _(pe):
            def fill(plan, first):
                for n, (kind, j) in enumerate(plan, first):
                    if n >= RING:
                        pe.wait_ge(prep_sb, n - RING + 1)
                    ps = prep_bank(n)
                    if kind == "w2T":
                        for i in range(j, min(j + W_AT_ONCE, F)):
                            last = nc.tensor.transpose(ps[:, (i - j) * P:(i - j + 1) * P], w2[:, :, i], ident[:, :])
                    elif kind == "d":
                        pe.wait_ge(dn_in, 16)
                        for t in range(T):
                            last = nc.tensor.transpose(ps[0:DC, t * P:(t + 1) * P], dn[:, t, :], ident[:, :])
                    elif kind == "D":
                        if j == 0:
                            pe.wait_ge(prep_sb, N_W2T)
                            pe.wait_ge(s_ready, 1)
                            pe.wait_ge(b1_in, 16)
                        last = nc.tensor.matmul(ps[:, 0:ND], w2T[:, j, :], S[:, :], start=True, stop=True)
                    elif kind == "w1":
                        for s in range(j, min(j + W_AT_ONCE, JG)):
                            k = g_rows(s) * F
                            src = w1[:, :, :].rearrange("h i j -> h (i j)")[:, 4 * s * F:4 * s * F + k]
                            last = nc.tensor.transpose(ps[0:k, (s - j) * P:(s - j + 1) * P], src, ident[:, :])
                    else:
                        lo, m = {"VA": (0, NP + 1), "VB": (DB, NP)}[kind]
                        for i in range(j, min(j + W_AT_ONCE, F)):
                            last = nc.tensor.transpose(ps[0:m, (i - j) * P:(i - j + 1) * P], D[:, i, lo:lo + m],
                                                       ident[:, :])
                    last.then_inc(prep_ps, 1)

            def moments(t):
                pe.wait_ge(pair_ok, t + 1)
                pe.wait_ge(bd_ok, t + 1)
                for n in range(UNITS):
                    u = UNITS * t + n
                    if u >= RING:
                        pe.wait_ge(c_sb, u - RING + 1)
                    lo, m = ((0, MA), (PB, NP))[n % 2]
                    for i in range(GP):
                        g = (n // 2) * GP + i
                        last = nc.tensor.matmul(bank[u % RING][0:m, i * Q * F:(i + 1) * Q * F],
                                                PT[t % 2][:, lo:lo + m, g], BD[t % 2][:, g, :], start=True, stop=True)
                    last.then_inc(c_ps, 1)

            def final(t):
                pe.wait_ge(c_sb, UNITS * (t + 1))
                if t == 0:
                    pe.wait_ge(prep_sb, len(prep) + len(prep_late))
                if t >= 2:
                    pe.wait_ge(z_ok, t - 1)
                zb = bank[4 + t % 2]
                for j in range(F):
                    nc.tensor.matmul(zb[:, 0:P], VA[:, j, :], CA[t % 2][0:NP + 1, j, :], start=(j == 0), stop=False)
                    nc.tensor.matmul(zb[:, 0:P], VB[:, j, :], CB[t % 2][0:NP, j, :], start=False, stop=(j == F - 1))
                pe.wait_ge(g_in[t % 2], 64 * (t // 2 + 1))
                for s in range(JG):
                    k = g_rows(s) * F
                    last = nc.tensor.matmul(zb[:, P:2 * P], W1G[0:k, s, :], G4[t % 2][0:k, s, :],
                                            start=(s == 0), stop=(s == JG - 1))
                last.then_inc(f_done, 1)

            def layer1(t):
                pe.wait_ge(z_ok, t + 1)
                if t == 0:
                    pe.wait_ge(top_in, 16 * 6)
                if t >= 1:
                    pe.wait_ge(l1_ok, t)
                for c in range(C1):
                    dst = bank[6][:, c * P:(c + 1) * P]
                    for i in range(2):
                        nc.tensor.matmul(dst, wt1[:, i, c::C1], z[t % 2][:, i, :], start=(i == 0), stop=False)
                    last = nc.tensor.matmul(dst, wt1d[:, c::C1], dT[:, t, :], start=False, stop=True)
                last.then_inc(l1_ps, 1)

            def layer2(t):
                pe.wait_ge(l1_ok, t + 1)
                if t >= 1:
                    pe.wait_ge(l2_ok, t)
                for c in range(C2):
                    for i in range(C1):
                        last = nc.tensor.matmul(bank[7][:, c * P:(c + 1) * P], wt2[:, i, c::C2], h1[t % 2][:, i, :],
                                                start=(i == 0), stop=(i == C1 - 1))
                last.then_inc(l2_ps, 1)

            def layer3(t):
                pe.wait_ge(l2_ok, t + 1)
                if t >= 1:
                    pe.wait_ge(y_ok, t)
                for i in range(C2):
                    last = nc.tensor.matmul(bank[7][0:1, 2 * P:3 * P], wt3[:, i:i + 1], h2[t % 2][:, i, :],
                                            start=(i == 0), stop=(i == C2 - 1))
                last.then_inc(l3_ps, 1)

            pe.wait_ge(ident_ok, 1)
            pe.wait_ge(w2_in, 16)
            pe.wait_ge(w1_in, 16)
            fill(prep, 0)
            moments(0)
            pe.wait_ge(sym_ok, 1)
            fill(prep_late, len(prep))
            for t in range(1, T):
                final(t - 1)
                if t >= 2:
                    layer1(t - 2)
                moments(t)
                if t >= 2:
                    layer2(t - 2)
                    layer3(t - 2)
            layer1(T - 2)
            final(T - 1)
            layer2(T - 2)
            layer3(T - 2)
            layer1(T - 1)
            layer2(T - 1)
            layer3(T - 1)


def kernel(**inputs):
    import numpy as _np
    import concourse.bacc as _bacc
    from concourse import mybir as _mybir
    from concourse.bass_utils import run_bass_kernel_spmd as _run

    nc = _bacc.Bacc("TRN2", target_bir_lowering=False, num_devices=1)
    arrays, args = {}, {}
    for name in inputs:
        a = _np.ascontiguousarray(inputs[name])
        arrays[f"in_{name}_dram"] = a
        args[name] = nc.dram_tensor(f"in_{name}_dram", a.shape, _mybir.dt.from_np(a.dtype), kind="ExternalInput").ap()
    rows = inputs["ids"].shape[0]
    out = nc.dram_tensor("out_0_dram", (rows, 1), _mybir.dt.float32, kind="ExternalOutput").ap()
    dlrm_cin_tower(nc, args, out)
    r = _run(nc, [arrays], core_ids=[0])
    return r.results[0]["out_0_dram"]
```

```python
import concourse.bass as bass
from concourse import mybir
from contextlib import ExitStack


def dlrm_cin_tower(nc, x, out):
    fp32 = mybir.dt.float32
    i32 = mybir.dt.int32
    ALU = mybir.AluOpType
    ACT = mybir.ActivationFunctionType

    P = 128
    B, F = x["ids"].shape
    K = x["tbl_0"].shape[1]
    H = x["L0_rec_W1"].shape[0]
    DC = x["dense_ctx"].shape[1]
    O1 = x["W_top2"].shape[0]
    O2 = x["W_top3"].shape[0]
    T = B // P
    Q = P // K
    NG = P // Q
    HF = F // 2
    OFF = HF * (HF - 1) // 2
    NP = HF + OFF
    ONE = OFF
    EF = NP + 1
    MA = EF + F
    PB = MA
    NS = MA + NP
    DB = NP + 1
    DX = DB + NP
    ND = DX + HF * HF
    GP = 4
    NB = NG // GP
    RING = 4
    JG = -(-F // 4)
    W_AT_ONCE = 4
    C1, C2 = O1 // P, O2 // P

    PARTS = [0, HF, F - 6, F - 2, F]

    NPART = len(PARTS) - 1

    MC = HF - HF // 2

    def off(n):
        return OFF - n * (n + 1) // 2

    def run(n, half):
        return off(n), OFF - off(n) + 1 - half + n + 1

    def moved_to(n, half):
        return (MA, NP)[half] if n == 0 else 0

    ROWS = (NP + 1, NP)
    TALL = (MA + run(0, 0)[1], NP + run(0, 1)[1])
    SQ = (ONE + 1, OFF)
    COLS = HF + MC

    ctx = ExitStack()
    with ctx:
        def sb(name, shape, dt=fp32):
            return ctx.enter_context(nc.sbuf_tensor(name, shape, dt))

        def sem(name):
            return ctx.enter_context(nc.semaphore(name))

        idx = sb("idx", [P, T, F], i32)
        E = sb("E", [P, T, F, K])
        late = sb("late", [P, NS * NG + 2 * JG * P + 2 * (2 + C1 + C2) * P])
        taken = [0]

        def part(n):
            taken[0] += n * P
            return late[:, taken[0] - n * P:taken[0]].rearrange("p (n b) -> p n b", b=P)

        D = late[:, 0:F * ND].rearrange("p (j n) -> p j n", n=ND)
        PT1 = late[:, 0:NS * NG].rearrange("p (s g) -> p s g", g=NG)
        taken[0] = NS * NG
        PT = [sb("PT0", [P, NS, NG]), PT1]
        BD = [sb(f"BD{i}", [P, NG, Q * F]) for i in range(2)]
        CA = [sb(f"CA{i}", [P, F, P]) for i in range(2)]
        CB = [sb(f"CB{i}", [P, F, P]) for i in range(2)]
        G4 = [part(JG) for i in range(2)]
        w1 = sb("w1", [H, F, F])
        w2 = CA[1][:, :, :].rearrange("p a b -> p (a b)").rearrange("p (m j) -> p m j", j=F)
        w2T = CB[1]
        VP = []
        for rows in TALL:
            at = sum(v.shape[1] * v.shape[2] for v in VP)
            VP.append(CA[1][:, :, :].rearrange("p a b -> p (a b)")[:, at:at + HF * rows].rearrange(
                "p (j n) -> p j n", n=rows))
        PS = CB[1][:, :, :].rearrange("p a b -> p (a b)")[:, 0:HF ** 3].rearrange("p (j y x) -> p j y x", y=HF, x=HF)
        S = sb("S", [H, ND])
        V = [sb("VA", [TALL[0], COLS, H]), sb("VB", [TALL[1], COLS, H])]
        W1G = sb("W1G", [4 * F, JG, H])
        ident = sb("ident", [P, P])
        wt1 = sb("wt1", [P, 2, O1])
        wt1d = sb("wt1d", [DC, O1])
        wt2 = sb("wt2", [P, C1, O2])
        wt3 = sb("wt3", [P, C2])
        bt1 = sb("bt1", [P, C1])
        bt2 = sb("bt2", [P, C2])
        b12 = sb("b12", [P, 2])
        b12k = sb("b12k", [P, 2])
        dn = sb("dn", [P, T, DC])
        dT = sb("dT", [DC, T, P])
        z = [part(2) for i in range(2)]
        h1 = [part(C1) for i in range(2)]
        h2 = [part(C2) for i in range(2)]
        y = sb("y", [1, T, P])
        bank = [ctx.enter_context(nc.psum_tensor(f"bank{i}", [P, 512], fp32)) for i in range(8)]

        ids_in, w1_in, w2_in, b12_in, b1_in = sem("ids_in"), sem("w1_in"), sem("w2_in"), sem("b12_in"), sem("b1_in")
        top_in, dn_in = sem("top_in"), sem("dn_in")
        gathered = [[sem(f"gathered{t}_{p}") for p in range(len(PARTS) - 1)] for t in range(T)]
        ident_zero, ident_ok = sem("ident_zero"), sem("ident_ok")
        b12k_ok = sem("b12k_ok")
        s_ready = sem("s_ready")
        prep_ps = sem("prep_ps")
        prep_sb = sem("prep_sb")
        cross_ok = sem("cross_ok")
        inner_ok = sem("inner_ok")
        chain = sem("chain")
        e_ok = sem("e_ok")
        bd_ok = sem("bd_ok")
        pair_ok = sem("pair_ok")
        c_ps = sem("c_ps")
        c_sb = sem("c_sb")
        g_in = [sem(f"g_in{i}") for i in range(2)]
        m_in = [[sem(f"m_in{h}_{i}") for i in range(2)] for h in range(2)]
        f_done = sem("f_done")
        z_ok = sem("z_ok")
        l1_ps, l1_ok = sem("l1_ps"), sem("l1_ok")
        l2_ps, l2_ok = sem("l2_ps"), sem("l2_ok")
        l3_ps, y_ok, y_out = sem("l3_ps"), sem("y_ok"), sem("y_out")

        W1_SLOTS = list(range(0, JG - 1, W_AT_ONCE)) + [JG - 1]
        prep = ([("w1", s) for s in W1_SLOTS] + [("d", 0)] + [("w2T", j) for j in range(0, F, W_AT_ONCE)] + [("D", j) for j in range(F)])
        late_cross = [(h, c) for h in range(2) for c in range(0, HF, W_AT_ONCE)]
        late_inner = [(h, c) for h in range(2) for c in list(range(HF, COLS - 1, W_AT_ONCE)) + [COLS - 1]]
        N_CROSS = len(prep) + len(late_cross)
        N_ALL = N_CROSS + len(late_inner)
        N_W2T = len(prep) - F
        UNITS = 2 * NB
        MOVES = HF // 2

        def prep_bank(n):
            return bank[4 + n % RING] if n < N_CROSS else bank[6 + n % 2]

        def prep_free(n):
            return n - (RING if n < N_CROSS else 2) + 1

        def w1_slots(s):
            return 1 if s == JG - 1 else min(W_AT_ONCE, JG - 1 - s)

        def late_cols(c):
            return min(W_AT_ONCE, (HF if c < HF else COLS - 1 if c < COLS - 1 else COLS) - c)

        def late_rows(h, c):
            return TALL[h] if c == COLS - 1 else ROWS[h]

        def g_rows(s):
            return min(4, F - 4 * s)

        block = ctx.enter_context(nc.Block())

        @block.sync
        def _(sp):
            sp.dma_start(idx[:, :, :], x["ids"].rearrange("(t p) f -> p t f", p=P)).then_inc(ids_in, 16)
            sp.dma_start(w1[:, :, :], x["L0_rec_W1"][:, :, :]).then_inc(w1_in, 16)
            sp.dma_start(w2[:, :, :], x["L0_rec_W2"][:, :, :]).then_inc(w2_in, 16)
            b1c = x["L0_rec_b1"].rearrange("(h o) -> h o", o=1)
            b2c = x["L0_rec_b2"].rearrange("(h o) -> h o", o=1)
            sp.dma_start(S[:, ONE:ONE + 1], b1c).then_inc(b1_in, 16)
            sp.dma_start(b12[:, 0:1], b1c).then_inc(b12_in, 16)
            sp.dma_start(b12[:, 1:2], b2c).then_inc(b12_in, 16)
            sp.dma_start(dn[:, :, :], x["dense_ctx"].rearrange("(t p) c -> p t c", p=P)).then_inc(dn_in, 16)
            sp.dma_start(wt1[:, :, :], x["W_top1"][0:2 * P, :].rearrange("(c p) o -> p c o", p=P)).then_inc(top_in, 16)
            sp.dma_start(wt1d[:, :], x["W_top1"][2 * P:, :]).then_inc(top_in, 16)
            sp.dma_start(wt2[:, :, :], x["W_top2"].rearrange("(p c) o -> p c o", c=C1)).then_inc(top_in, 16)
            sp.dma_start(wt3[:, :], x["W_top3"].rearrange("(p c) o -> p (c o)", c=C2)).then_inc(top_in, 16)
            sp.dma_start(bt1[:, :], x["b_top1"].rearrange("(p c) -> p c", c=C1)).then_inc(top_in, 16)
            sp.dma_start(bt2[:, :], x["b_top2"].rearrange("(p c) -> p c", c=C2)).then_inc(top_in, 16)
            for t in range(T):
                C = (CA[t % 2], CB[t % 2])
                for half in range(2):
                    sp.wait_ge(c_sb, UNITS * t + NB * (half + 1))
                    for n in range(MOVES):
                        r0, k = run(n, half)
                        r1, c = moved_to(n, half), half * HF
                        sp.dma_start(C[half][r1:r1 + k, c + HF - 1 - n, :],
                                     C[half][r0:r0 + k, c + n, :]).then_inc(m_in[half][t % 2], 16)
                if t == 0:
                    sp.wait_ge(prep_ps, N_ALL)
                if t >= 2:
                    sp.wait_ge(f_done, t - 1)
                for q in range(4):
                    n = len(range(q, F, 4))
                    sp.dma_start(G4[t % 2][q * F:(q + 1) * F, 0:n, :],
                                 CA[t % 2][EF:EF + F, q::4, :]).then_inc(g_in[t % 2], 16)
            sp.wait_ge(y_ok, T)
            sp.dma_start(out.rearrange("b o -> o b"), y[:, :, :].rearrange("o t p -> o (t p)")).then_inc(y_out, 16)
            sp.wait_ge(y_out, 16)

        @block.gpsimd
        def _(pool):
            nc.gpsimd.memset(ident[:, :], 0.0).then_inc(ident_zero, 1)
            pool.wait_ge(ident_zero, 1)
            nc.gpsimd.affine_select(out=ident[:, :], in_=ident[:, :], compare_op=ALU.not_equal, fill=1.0, base=0,
                                    pattern=[[-1, P]], channel_multiplier=1).then_inc(ident_ok, 1)
            pool.wait_ge(ids_in, 16)
            for t in range(T):
                for p, (lo, hi) in enumerate(zip(PARTS, PARTS[1:])):
                    for f in range(lo, hi):
                        pool.indirect_dma_start(
                            out=E[:, t, f, :], out_offset=None, in_=x[f"tbl_{f}"][:, :],
                            in_offset=bass.IndirectOffsetOnAxis(ap=idx[:, t, f:f + 1], axis=0),
                        ).then_inc(gathered[t][p], 16)

        @block.vector
        def _(dve):
            links = [0]

            def link(ins):
                links[0] += 1
                ins.then_inc(chain, 1)
                dve.wait_ge(chain, links[0])

            for i in range(2):
                nc.vector.memset(BD[i][:, :, :], 0.0)
            dve.wait_ge(w1_in, 16)
            wf = w1[:, :, :].rearrange("p i j -> p (i j)")
            for half, base, sq in ((0, 0, SQ[0]), (HF, DB, DB + SQ[1])):
                d0 = half * (F + 1)
                nc.vector.tensor_copy(S[:, sq:sq + HF], wf[:, d0:d0 + (HF - 1) * (F + 1) + 1:F + 1])
                for n in range(1, HF):
                    nc.vector.tensor_tensor(S[:, base + off(n):base + off(n) + n], w1[:, half:half + n, half + n],
                                            w1[:, half + n, half:half + n], ALU.add)
            nc.vector.tensor_tensor(S[:, DX:].rearrange("p (a b) -> p a b", b=HF), w1[:, 0:HF, HF:],
                                    w1[:, HF:, 0:HF].rearrange("p b a -> p a b"), ALU.add).then_inc(s_ready, 1)
            dve.wait_ge(b12_in, 32)
            nc.vector.tensor_scalar(b12k[:, :], b12[:, :], float(K), None, ALU.mult).then_inc(b12k_ok, 1)

            def pairs(t):
                buf = PT[t % 2]
                if t == 1:
                    dve.wait_ge(prep_ps, N_ALL)
                if t >= 2:
                    dve.wait_ge(c_ps, UNITS * (t - 1))
                if t < 2:
                    nc.vector.memset(buf[:, ONE, :], 1.0)
                for p, (lo, hi) in enumerate(zip(PARTS, PARTS[1:])):
                    dve.wait_ge(gathered[t][p], 16 * (hi - lo))
                    nc.vector.transpose(buf[:, EF + lo:EF + hi, :].rearrange("p f g -> p (f g)"),
                                        E[:, t, lo:hi, :].rearrange("p f k -> p (f k)")).then_inc(e_ok, 1)
                    dve.wait_ge(e_ok, t * NPART + p + 1)
                    for q in range(Q):
                        rows = slice(q * K, (q + 1) * K)
                        last = nc.vector.tensor_copy(BD[t % 2][rows, :, q * F + lo:q * F + hi],
                                                     buf[rows, EF + lo:EF + hi, :].rearrange("p f g -> p g f"))
                    if hi == F:
                        last.then_inc(bd_ok, 1)
                    first, base = (EF, 0) if hi <= HF else (EF + HF, PB)
                    a, b = (lo, hi) if hi <= HF else (lo - HF, hi - HF)
                    e = buf[:, first:first + HF, :]
                    sq = base + SQ[base > 0]
                    last = nc.vector.tensor_tensor(buf[:, sq + a:sq + b, :], e[:, a:b, :], e[:, a:b, :], ALU.mult)
                    for n in range(max(a, 1), b):
                        last = nc.vector.tensor_tensor(buf[:, base + off(n):base + off(n) + n, :], e[:, 0:n, :],
                                                       e[:, n:n + 1, :].to_broadcast([P, n, NG]), ALU.mult)
                    last.then_inc(pair_ok, 1)

            Df = D[:, :, :].rearrange("p j n -> p (j n)")

            def add_cross():
                dve.wait_ge(prep_sb, len(prep))
                X = D[:, :, DX:].rearrange("p j (a b) -> p j a b", b=HF)
                sa, sb_ = SQ[0], DB + SQ[1]
                last = None
                a, b = D[:, HF:, sa:sa + HF], D[:, 0:HF, sb_:sb_ + HF]
                xa = Df[:, DX:DX + HF * (ND + HF)].rearrange("p (n w) -> p n w", w=ND + HF)[:, :, 0:HF]
                at = HF * ND + DX
                xb = late[:, at:at + HF * (ND + 1)].rearrange("p (n w) -> p n w", w=ND + 1)[:, :, 0:HF * HF:HF]
                nc.vector.tensor_tensor(a, a, xa.rearrange("p n b -> p b n"), ALU.add)
                nc.vector.tensor_tensor(b, b, xb.rearrange("p n a -> p a n"), ALU.add)
                for order in range(2):
                    for n in range(1, HF):
                        a = D[:, HF:, off(n):off(n) + n]
                        b = D[:, 0:HF, DB + off(n):DB + off(n) + n]
                        xa, xb = ((X[:, 0:n, n, :].rearrange("p x b -> p b x"),
                                   X[:, HF:HF + n, :, n].rearrange("p x a -> p a x")),
                                  (X[:, n, 0:n, :].rearrange("p x b -> p b x"), X[:, HF + n, :, 0:n]))[order]
                        nc.vector.tensor_tensor(a, a, xa, ALU.add)
                        last = nc.vector.tensor_tensor(b, b, xb, ALU.add)
                    if order == 0:
                        link(last)
                last.then_inc(cross_ok, 1)

            def inner():
                for h, (j0, base) in enumerate(((0, 0), (HF, DB))):
                    link(nc.vector.memset(VP[h][:, HF - MC:, :], 0.0))
                for h, (j0, base) in enumerate(((0, 0), (HF, DB))):
                    vp, sq = VP[h], SQ[h]
                    vf = vp.rearrange("p j n -> p (j n)")
                    for n in range(1, HF):
                        run_n = D[:, j0:j0 + n, base + off(n):base + off(n) + n]
                        last = nc.vector.tensor_tensor(PS[:, n, 0:n, 0:n], run_n, run_n.rearrange("p y x -> p x y"),
                                                       ALU.add)
                        nc.vector.tensor_tensor(vp[:, n, off(n):off(n) + n], D[:, j0 + n, base + off(n):base + off(n) + n],
                                                D[:, j0:j0 + n, base + sq + n], ALU.add)
                        first = j0 * ND + base + off(n)
                        nc.vector.tensor_tensor(vp[:, n, sq:sq + n], D[:, j0 + n, base + sq:base + sq + n],
                                                Df[:, first:first + (n - 1) * (ND + 1) + 1:ND + 1], ALU.add)
                    link(last)
                    for n in range(1, HF - 1):
                        nc.vector.tensor_tensor(vp[:, n + 1:, off(n):off(n) + n],
                                                D[:, j0 + n + 1:j0 + HF, base + off(n):base + off(n) + n],
                                                PS[:, n + 1:, n, 0:n], ALU.add)
                    first = j0 * ND + base + sq
                    last = nc.vector.tensor_copy(vf[:, sq::TALL[h] + 1][:, 0:HF],
                                                 Df[:, first:first + (HF - 1) * (ND + 1) + 1:ND + 1])
                    if h == 0:
                        last = nc.vector.tensor_copy(vp[:, :, ONE], D[:, 0:HF, ONE])
                    link(last)
                    for n in range(MOVES):
                        r0, k = run(n, h)
                        r1 = moved_to(n, h)
                        last = nc.vector.tensor_copy(vp[:, HF - 1 - n, r1:r1 + k], vp[:, n, r0:r0 + k])
                last.then_inc(inner_ok, 1)

            pairs(0)
            add_cross()
            inner()
            for t in range(1, T):
                pairs(t)

        @block.scalar
        def _(act):
            def empty(plan, first):
                for n, (kind, j) in enumerate(plan, first):
                    act.wait_ge(prep_ps, n + 1)
                    src = prep_bank(n)
                    if kind == "d":
                        dst, src = dT[:, :, :], src[0:DC, 0:T * P].rearrange("c (t p) -> c t p", p=P)
                    elif kind == "D":
                        dst, src = D[:, j, :], src[:, 0:ND]
                    elif kind == "w1":
                        m, rows = w1_slots(j), g_rows(j) * F
                        dst, src = W1G[0:rows, j:j + m, :], src[0:rows, 0:m * P].rearrange("p (j h) -> p j h", h=H)
                    else:
                        m = min(W_AT_ONCE, F - j)
                        dst, src = w2T[:, j:j + m, :], src[:, 0:m * P].rearrange("p (j h) -> p j h", h=H)
                    nc.scalar.copy(dst, src).then_inc(prep_sb, 1)

            def empty_late(plan, first):
                for n, (h, c) in enumerate(plan, first):
                    act.wait_ge(prep_ps, n + 1)
                    m, rows = late_cols(c), late_rows(h, c)
                    nc.scalar.copy(V[h][0:rows, c:c + m, :], prep_bank(n)[0:rows, 0:m * P].rearrange(
                        "p (j h) -> p j h", h=H)).then_inc(prep_sb, 1)

            def moments(t):
                if t >= 2:
                    act.wait_ge(f_done, t - 1)
                for n in range(UNITS):
                    u = UNITS * t + n
                    act.wait_ge(c_ps, u + 1)
                    C, rows = ((CA, MA), (CB, NP))[n // NB]
                    g0 = (n % NB) * GP
                    dst = C[t % 2][0:rows, :, :].rearrange("s j (q g) -> s g q j", q=Q)[:, g0:g0 + GP, :, :]
                    src = bank[u % RING][0:rows, 0:GP * Q * F].rearrange("s (g q j) -> s g q j", g=GP, q=Q)
                    nc.scalar.copy(dst, src).then_inc(c_sb, 1)

            def z_out(t):
                act.wait_ge(f_done, t + 1)
                if t == 0:
                    act.wait_ge(b12k_ok, 1)
                if t >= 2:
                    act.wait_ge(l1_ps, t - 1)
                zb = bank[4 + t % 2]
                nc.scalar.activation(z[t % 2][:, 0, :], zb[:, P:2 * P], ACT.Identity, bias=b12k[:, 0:1])
                nc.scalar.activation(z[t % 2][:, 1, :], zb[:, 0:P], ACT.Identity, bias=b12k[:, 1:2]).then_inc(z_ok, 1)

            def relu(dst, src, bias, n):
                for c in range(n):
                    last = nc.scalar.activation(dst[:, c, :], src[:, c * P:(c + 1) * P], ACT.Relu,
                                                bias=bias[:, c:c + 1])
                return last

            def l1_out(t):
                act.wait_ge(l1_ps, t + 1)
                if t == 0:
                    act.wait_ge(top_in, 16 * 6)
                if t >= 2:
                    act.wait_ge(l2_ps, t - 1)
                relu(h1[t % 2], bank[6], bt1, C1).then_inc(l1_ok, 1)

            def l2_out(t):
                act.wait_ge(l2_ps, t + 1)
                if t >= 2:
                    act.wait_ge(l3_ps, t - 1)
                relu(h2[t % 2], bank[7], bt2, C2).then_inc(l2_ok, 1)

            def l3_out(t):
                act.wait_ge(l3_ps, t + 1)
                nc.scalar.copy(y[:, t, :], bank[7][0:1, 2 * P:3 * P]).then_inc(y_ok, 1)

            empty(prep, 0)
            moments(0)
            empty_late(late_cross, len(prep))
            empty_late(late_inner, N_CROSS)
            for t in range(1, T):
                z_out(t - 1)
                moments(t)
                l1_out(t - 1)
                l2_out(t - 1)
                l3_out(t - 1)
            z_out(T - 1)
            l1_out(T - 1)
            l2_out(T - 1)
            l3_out(T - 1)

        @block.tensor
        def _(pe):
            def fill(plan, first):
                for n, (kind, j) in enumerate(plan, first):
                    if n >= RING:
                        pe.wait_ge(prep_sb, n - RING + 1)
                    ps = prep_bank(n)
                    if kind == "w2T":
                        pe.wait_ge(w2_in, 16)
                        for i in range(j, min(j + W_AT_ONCE, F)):
                            last = nc.tensor.transpose(ps[:, (i - j) * P:(i - j + 1) * P], w2[:, :, i], ident[:, :])
                    elif kind == "d":
                        pe.wait_ge(dn_in, 16)
                        for t in range(T):
                            last = nc.tensor.transpose(ps[0:DC, t * P:(t + 1) * P], dn[:, t, :], ident[:, :])
                    elif kind == "D":
                        if j == 0:
                            pe.wait_ge(prep_sb, N_W2T)
                            pe.wait_ge(s_ready, 1)
                            pe.wait_ge(b1_in, 16)
                        last = nc.tensor.matmul(ps[:, 0:ND], w2T[:, j, :], S[:, :], start=True, stop=True)
                    elif kind == "w1":
                        for s in range(j, j + w1_slots(j)):
                            k = g_rows(s) * F
                            src = w1[:, :, :].rearrange("h i j -> h (i j)")[:, 4 * s * F:4 * s * F + k]
                            last = nc.tensor.transpose(ps[0:k, (s - j) * P:(s - j + 1) * P], src, ident[:, :])
                    last.then_inc(prep_ps, 1)

            def fill_late(plan, first):
                for n, (h, c) in enumerate(plan, first):
                    pe.wait_ge(prep_sb, prep_free(n))
                    rows = late_rows(h, c)
                    for i in range(late_cols(c)):
                        if c < HF:
                            src = D[:, (1 - h) * HF + c + i, h * DB:h * DB + rows]
                        else:
                            src = VP[h][:, c + i - HF + HF - MC, 0:rows]
                        last = nc.tensor.transpose(prep_bank(n)[0:rows, i * P:(i + 1) * P], src, ident[:, :])
                    last.then_inc(prep_ps, 1)

            def moments(t):
                pe.wait_ge(pair_ok, NPART * t + 1)
                pe.wait_ge(bd_ok, t + 1)
                for n in range(UNITS):
                    u = UNITS * t + n
                    if n == NB:
                        pe.wait_ge(pair_ok, NPART * (t + 1))
                    if u >= RING:
                        pe.wait_ge(c_sb, u - RING + 1)
                    lo, m = ((0, MA), (PB, NP))[n // NB]
                    for i in range(GP):
                        g = (n % NB) * GP + i
                        last = nc.tensor.matmul(bank[u % RING][0:m, i * Q * F:(i + 1) * Q * F],
                                                PT[t % 2][:, lo:lo + m, g], BD[t % 2][:, g, :], start=True, stop=True)
                    last.then_inc(c_ps, 1)

            def final_cross(t, h):
                pe.wait_ge(c_sb, UNITS * t + NB * (h + 1))
                if h == 0 and t == 0:
                    pe.wait_ge(prep_sb, N_CROSS)
                if h == 0 and t >= 2:
                    pe.wait_ge(z_ok, t - 1)
                for j in range(HF):
                    nc.tensor.matmul(bank[4 + t % 2][:, 0:P], V[h][0:ROWS[h], j, :],
                                     (CA, CB)[h][t % 2][0:ROWS[h], (1 - h) * HF + j, :],
                                     start=(h == 0 and j == 0), stop=False)

            def final_inner(t, h):
                pe.wait_ge(m_in[h][t % 2], 16 * MOVES * (t // 2 + 1))
                if h == 0 and t == 0:
                    pe.wait_ge(prep_sb, N_ALL)
                for j in range(MC):
                    rows = TALL[h] if j == MC - 1 else ROWS[h]
                    nc.tensor.matmul(bank[4 + t % 2][:, 0:P], V[h][0:rows, HF + j, :],
                                     (CA, CB)[h][t % 2][0:rows, h * HF + HF - MC + j, :],
                                     start=False, stop=(h == 1 and j == MC - 1))

            def final_g(t):
                pe.wait_ge(g_in[t % 2], 64 * (t // 2 + 1))
                for s in range(JG):
                    k = g_rows(s) * F
                    last = nc.tensor.matmul(bank[4 + t % 2][:, P:2 * P], W1G[0:k, s, :], G4[t % 2][0:k, s, :],
                                            start=(s == 0), stop=(s == JG - 1))
                last.then_inc(f_done, 1)

            def layer1(t):
                pe.wait_ge(z_ok, t + 1)
                if t == 0:
                    pe.wait_ge(top_in, 16 * 6)
                if t >= 1:
                    pe.wait_ge(l1_ok, t)
                for c in range(C1):
                    dst = bank[6][:, c * P:(c + 1) * P]
                    for i in range(2):
                        nc.tensor.matmul(dst, wt1[:, i, c::C1], z[t % 2][:, i, :], start=(i == 0), stop=False)
                    last = nc.tensor.matmul(dst, wt1d[:, c::C1], dT[:, t, :], start=False, stop=True)
                last.then_inc(l1_ps, 1)

            def layer2(t):
                pe.wait_ge(l1_ok, t + 1)
                if t >= 1:
                    pe.wait_ge(l2_ok, t)
                for c in range(C2):
                    for i in range(C1):
                        last = nc.tensor.matmul(bank[7][:, c * P:(c + 1) * P], wt2[:, i, c::C2], h1[t % 2][:, i, :],
                                                start=(i == 0), stop=(i == C1 - 1))
                last.then_inc(l2_ps, 1)

            def layer3(t):
                pe.wait_ge(l2_ok, t + 1)
                if t >= 1:
                    pe.wait_ge(y_ok, t)
                for i in range(C2):
                    last = nc.tensor.matmul(bank[7][0:1, 2 * P:3 * P], wt3[:, i:i + 1], h2[t % 2][:, i, :],
                                            start=(i == 0), stop=(i == C2 - 1))
                last.then_inc(l3_ps, 1)

            pe.wait_ge(ident_ok, 1)
            pe.wait_ge(w1_in, 16)
            fill(prep, 0)
            moments(0)
            pe.wait_ge(cross_ok, 1)
            fill_late(late_cross, len(prep))
            final_cross(0, 0)
            final_cross(0, 1)
            pe.wait_ge(inner_ok, 1)
            fill_late(late_inner, N_CROSS)
            final_inner(0, 0)
            final_inner(0, 1)
            final_g(0)
            for t in range(1, T):
                moments(t)
                layer1(t - 1)
                final_cross(t, 0)
                final_cross(t, 1)
                layer2(t - 1)
                final_inner(t, 0)
                final_inner(t, 1)
                layer3(t - 1)
                final_g(t)
            layer1(T - 1)
            layer2(T - 1)
            layer3(T - 1)


def kernel(**inputs):
    import numpy as _np
    import concourse.bacc as _bacc
    from concourse import mybir as _mybir
    from concourse.bass_utils import run_bass_kernel_spmd as _run

    nc = _bacc.Bacc("TRN2", target_bir_lowering=False, num_devices=1)
    arrays, args = {}, {}
    for name in inputs:
        a = _np.ascontiguousarray(inputs[name])
        arrays[f"in_{name}_dram"] = a
        args[name] = nc.dram_tensor(f"in_{name}_dram", a.shape, _mybir.dt.from_np(a.dtype), kind="ExternalInput").ap()
    rows = inputs["ids"].shape[0]
    out = nc.dram_tensor("out_0_dram", (rows, 1), _mybir.dt.float32, kind="ExternalOutput").ap()
    dlrm_cin_tower(nc, args, out)
    r = _run(nc, [arrays], core_ids=[0])
    return r.results[0]["out_0_dram"]
```

```python
import concourse.bass as bass
from concourse import mybir
from contextlib import ExitStack


def dlrm_cin_tower(nc, x, out):
    fp32 = mybir.dt.float32
    fp32r = mybir.dt.float32r
    i32 = mybir.dt.int32
    ALU = mybir.AluOpType
    ACT = mybir.ActivationFunctionType

    P = 128
    B, F = x["ids"].shape
    K = x["tbl_0"].shape[1]
    H = x["L0_rec_W1"].shape[0]
    DC = x["dense_ctx"].shape[1]
    O1 = x["W_top2"].shape[0]
    O2 = x["W_top3"].shape[0]
    T = B // P
    Q = P // K
    NG = P // Q
    HF = F // 2
    OFF = HF * (HF - 1) // 2
    NP = HF + OFF
    ONE = OFF
    EA, EB = NP + 1, NP
    MA, MB = EA + HF, EB + HF
    PB = MA
    NS = MA + MB
    DB = NP + 1
    DX = DB + NP
    ND = DX + HF * HF
    GP = 4
    NB = NG // GP
    RING = 4
    GA, GB = 5, 3
    JG = (F - 1) // GA
    GBLK = GA + GB
    assert GA * JG == F - 1 and GB * (JG - 1) < HF <= GB * (JG - 1) + 1
    W_AT_ONCE = 4
    C1, C2 = O1 // P, O2 // P

    PARTS = [0, HF, F - 6, F - 2, F]

    NPART = len(PARTS) - 1
    PAIRS = 3

    MC = 5

    def off(n):
        return OFF - n * (n + 1) // 2

    def run(n, half):
        return off(n), OFF - off(n) + 1 - half + n + 1

    MOVES = [MC - 1] + list(range(MC, HF - MC))
    ROWS = (NP + 1, NP)
    TALL = [(MA, MB)[half] + run(MC - 1, half)[1] for half in range(2)]

    def moved_to(n, half):
        if n < MC:
            return HF - MC + n, (MA, MB)[half] + off(n) - off(MC - 1)
        return HF - MC + (HF - MC - 1 - n), 0

    assert max(TALL) <= P and all(run(n, 0)[1] <= off(moved_to(n, 0)[0]) for n in MOVES[1:])

    SQ = (ONE + 1, OFF)
    COLS = HF + MC

    ctx = ExitStack()
    with ctx:
        def sb(name, shape, dt=fp32):
            return ctx.enter_context(nc.sbuf_tensor(name, shape, dt))

        def sem(name):
            return ctx.enter_context(nc.semaphore(name))

        idx = sb("idx", [P, T, F], i32)
        E = sb("E", [P, T, F, K])
        late = sb("late", [P, F * ND + 2 * P])
        taken = [0]

        def part(n):
            taken[0] += n * P
            return late[:, taken[0] - n * P:taken[0]].rearrange("p (n b) -> p n b", b=P)

        D = late[:, 0:F * ND].rearrange("p (j n) -> p j n", n=ND)
        PT = sb("PT", [P, NS, NG])
        BD = [sb(f"BD{i}", [P, NG, Q * F]) for i in range(2)]
        with ExitStack() as early:
            w2T = [early.enter_context(nc.sbuf_tensor(f"w2T{i}", [H, F, H], fp32r)) for i in range(2)]
            SR = [early.enter_context(nc.sbuf_tensor(f"SR{i}", [H, ND], fp32r)) for i in range(2)]
        CA = [sb("CA0", [P, F, P])]
        CB = [sb("CB0", [P, F, P])]
        G4 = [sb(f"G4{i}", [GBLK * HF, JG, P]) for i in range(2)]
        CA.append(sb("CA1", [P, F, P]))
        CB.append(sb("CB1", [P, F, P]))
        w1 = sb("w1", [H, F, F])
        w2 = CA[1][:, :, :].rearrange("p a b -> p (a b)").rearrange("p (m j) -> p m j", j=F)
        VP = []
        for rows in TALL:
            at = sum(v.shape[1] * v.shape[2] for v in VP)
            VP.append(CA[1][:, :, :].rearrange("p a b -> p (a b)")[:, at:at + HF * rows].rearrange(
                "p (j n) -> p j n", n=rows))
        PS = CB[1][:, :, :].rearrange("p a b -> p (a b)")[:, 0:HF ** 3].rearrange("p (j y x) -> p j y x", y=HF, x=HF)
        S = sb("S", [H, ND])
        V = [sb("VA", [TALL[0], COLS, H]), sb("VB", [TALL[1], COLS, H])]
        SG = CB[1][:, :, :].rearrange("p a b -> p (a b)")[:, HF ** 3:HF ** 3 + JG * GBLK * HF].rearrange(
            "p (s q i) -> p s q i", q=GBLK, i=HF)
        W1G = sb("W1G", [GBLK * HF, JG, H])
        ident = sb("ident", [P, P])
        wt1 = sb("wt1", [P, 2, O1])
        wt1d = sb("wt1d", [DC, O1])
        wt2 = sb("wt2", [P, C1, O2])
        wt3 = sb("wt3", [P, C2])
        bt1 = sb("bt1", [P, C1])
        bt2 = sb("bt2", [P, C2])
        b12 = sb("b12", [P, 2])
        b12k = sb("b12k", [P, 2])
        dn = sb("dn", [P, T, DC])
        dT = late[0:DC, 0:T * P]
        hd = sb("hd", [P, C1, T, P])
        z = part(2)
        h1 = part(C1)
        h2 = part(C2)
        y = part(T)[0:1, :, :]
        bank = [ctx.enter_context(nc.psum_tensor(f"bank{i}", [P, 512], fp32)) for i in range(8)]

        ids_in, w1_in, w2_in, b12_in, b1_in = sem("ids_in"), sem("w1_in"), sem("w2_in"), sem("b12_in"), sem("b1_in")
        top_in, dn_in, wt1d_in, bt1_in = sem("top_in"), sem("dn_in"), sem("wt1d_in"), sem("bt1_in")
        gathered = [[sem(f"gathered{t}_{p}") for p in range(len(PARTS) - 1)] for t in range(T)]
        ident_zero, ident_ok = sem("ident_zero"), sem("ident_ok")
        b12k_ok = sem("b12k_ok")
        s_ready = sem("s_ready")
        sg_ready = sem("sg_ready")
        prep_ps = sem("prep_ps")
        prep_sb = sem("prep_sb")
        low_ok = sem("low_ok")
        cross_ok = sem("cross_ok")
        inner_ok = sem("inner_ok")
        chain = sem("chain")
        e_ok = sem("e_ok")
        bd_zero = sem("bd_zero")
        bd_ok = sem("bd_ok")
        bd_last = sem("bd_last")
        pair_ok = sem("pair_ok")
        c_ps = sem("c_ps")
        c_sb = sem("c_sb")
        g_in = [sem(f"g_in{i}") for i in range(2)]
        g_in_pool = sem("g_in_pool")
        m_in = [[sem(f"m_in{h}_{i}") for i in range(2)] for h in range(2)]
        z2_ps = sem("z2_ps")
        f_done = sem("f_done")
        z2_ok, z1_ok = sem("z2_ok"), sem("z1_ok")
        l1_ps = sem("l1_ps")
        l1_sum = sem("l1_sum")
        l1_ok = sem("l1_ok")
        l2_ps = sem("l2_ps")
        l2_ok = sem("l2_ok")
        l3_ps = sem("l3_ps")
        y_ok = sem("y_ok")
        y_out = sem("y_out")

        W1_SLOTS = list(range(0, JG - 1, W_AT_ONCE)) + [JG - 1]
        prep = ([("d", 0)] + [("hd", c) for c in range(C1)] + [("w2T", j) for j in range(0, F, W_AT_ONCE)]
                + [("w1", s) for s in W1_SLOTS] + [("D", j) for j in range(F)])
        late_cross = [(h, c) for h in range(2) for c in range(0, HF, W_AT_ONCE)]
        late_inner = [(h, c) for h in range(2) for c in range(HF, COLS, W_AT_ONCE)]
        N_CROSS = len(prep) + len(late_cross)
        N_ALL = N_CROSS + len(late_inner)
        W2T_AT = 1 + C1
        N_W2T = W2T_AT + -(-F // W_AT_ONCE)
        UNITS = 2 * NB
        DENSE_FIRST = 2
        AT_L2, AT_L3 = 2, 2
        L2_BANK = (7, 6)
        CUT = UNITS - 1

        def prep_bank(n):
            return bank[4 + n % RING] if n < N_CROSS else bank[n - N_CROSS]

        def w1_slots(s):
            return 1 if s == JG - 1 else min(W_AT_ONCE, JG - 1 - s)

        def late_cols(c):
            return min(W_AT_ONCE, (HF if c < HF else COLS) - c)

        def late_rows(h, c):
            return TALL[h] if c >= HF else ROWS[h]

        def g_rows(s):
            return HF * (GBLK if s < JG - 1 else GA + 2)

        G_MOVES = GA + 1 + GB
        G_AHEAD = 5
        G_EARLY, G_LATE = list(range(G_AHEAD)), list(range(G_AHEAD, G_MOVES))

        def g_move(eng, t, n, done):
            if n == GA:
                eng.dma_start(G4[t % 2][(GA + 1) * HF:(GA + 2) * HF, JG - 1, :],
                              CA[t % 2][EA:EA + HF, F - 1, :]).then_inc(done, 16)
                return
            q = n if n < GA else n - GA - 1
            C, e, j, each, end = (CA, EA, 0, GA, F - 1) if n < GA else (CB, EB, HF, GB, F)
            slots = len(range(j + q, end, each))
            r = (n if n < GA else n - 1) * HF
            eng.dma_start(G4[t % 2][r:r + HF, 0:slots, :], C[t % 2][e:e + HF, j + q:end:each, :]).then_inc(done, 16)

        block = ctx.enter_context(nc.Block())

        @block.sync
        def _(sp):
            sp.dma_start(idx[:, :, :], x["ids"].rearrange("(t p) f -> p t f", p=P)).then_inc(ids_in, 16)
            sp.dma_start(dn[:, :, :], x["dense_ctx"].rearrange("(t p) c -> p t c", p=P)).then_inc(dn_in, 16)
            sp.dma_start(w2[:, :, :], x["L0_rec_W2"][:, :, :]).then_inc(w2_in, 16)
            sp.dma_start(w1[:, :, :], x["L0_rec_W1"][:, :, :]).then_inc(w1_in, 16)
            b1c = x["L0_rec_b1"].rearrange("(h o) -> h o", o=1)
            b2c = x["L0_rec_b2"].rearrange("(h o) -> h o", o=1)
            sp.dma_start(S[:, ONE:ONE + 1], b1c).then_inc(b1_in, 16)
            sp.dma_start(b12[:, 0:1], b1c).then_inc(b12_in, 16)
            sp.dma_start(b12[:, 1:2], b2c).then_inc(b12_in, 16)
            sp.dma_start(wt1[:, :, :], x["W_top1"][0:2 * P, :].rearrange("(c p) o -> p c o", p=P)).then_inc(top_in, 16)
            sp.dma_start(wt2[:, :, :], x["W_top2"].rearrange("(p c) o -> p c o", c=C1)).then_inc(top_in, 16)
            sp.dma_start(wt3[:, :], x["W_top3"].rearrange("(p c) o -> p (c o)", c=C2)).then_inc(top_in, 16)
            sp.dma_start(bt2[:, :], x["b_top2"].rearrange("(p c) -> p c", c=C2)).then_inc(top_in, 16)
            for t in range(T):
                C = (CA[t % 2], CB[t % 2])
                for half in range(2):
                    sp.wait_ge(c_sb, UNITS * t + NB * (half + 1))
                    for n in MOVES:
                        r0, k = run(n, half)
                        to, r1 = moved_to(n, half)
                        cols = MC if n < MC else 1
                        to, n = half * HF + to - cols + 1, half * HF + n - cols + 1
                        sp.dma_start(C[half][r1:r1 + k, to:to + cols, :],
                                     C[half][r0:r0 + k, n:n + cols, :]).then_inc(m_in[half][t % 2], 16)
                    if half == 0 and t >= 2:
                        sp.wait_ge(f_done, t - 1)
                    for n in G_EARLY if half == 0 else G_LATE if t < T - 1 else []:
                        g_move(sp, t, n, g_in[t % 2])
            sp.wait_ge(y_ok, T)
            sp.dma_start(out.rearrange("b o -> o b"), y[:, :, :].rearrange("o t p -> o (t p)")).then_inc(y_out, 16)
            sp.wait_ge(y_out, 16)

        @block.gpsimd
        def _(pool):
            nc.gpsimd.memset(ident[:, :], 0.0).then_inc(ident_zero, 1)
            pool.wait_ge(ident_zero, 1)
            nc.gpsimd.affine_select(out=ident[:, :], in_=ident[:, :], compare_op=ALU.not_equal, fill=1.0, base=0,
                                    pattern=[[-1, P]], channel_multiplier=1).then_inc(ident_ok, 1)
            pool.wait_ge(ids_in, 16)
            for t in range(T):
                for p, (lo, hi) in enumerate(zip(PARTS, PARTS[1:])):
                    for f in range(lo, hi):
                        pool.indirect_dma_start(
                            out=E[:, t, f, :], out_offset=None, in_=x[f"tbl_{f}"][:, :],
                            in_offset=bass.IndirectOffsetOnAxis(ap=idx[:, t, f:f + 1], axis=0),
                        ).then_inc(gathered[t][p], 16)
            t = T - 1
            pool.wait_ge(f_done, t - 1)
            pool.wait_ge(c_sb, UNITS * t + NB)
            for n in G_LATE[:-GB]:
                g_move(pool, t, n, g_in_pool)
            pool.wait_ge(c_sb, UNITS * T)
            for n in G_LATE[-GB:]:
                g_move(pool, t, n, g_in_pool)

        @block.vector
        def _(dve):
            links = [0]

            def link(ins):
                links[0] += 1
                ins.then_inc(chain, 1)
                dve.wait_ge(chain, links[0])

            nc.vector.memset(PT[:, ONE, :], 1.0)
            for i in range(2):
                nc.vector.memset(BD[i][:, :, :], 0.0).then_inc(bd_zero, 1)
            dve.wait_ge(w1_in, 16)
            wf = w1[:, :, :].rearrange("p i j -> p (i j)")
            for half, base, sq in ((0, 0, SQ[0]), (HF, DB, DB + SQ[1])):
                d0 = half * (F + 1)
                nc.vector.tensor_copy(S[:, sq:sq + HF], wf[:, d0:d0 + (HF - 1) * (F + 1) + 1:F + 1])
                for n in range(1, HF):
                    nc.vector.tensor_tensor(S[:, base + off(n):base + off(n) + n], w1[:, half:half + n, half + n],
                                            w1[:, half + n, half:half + n], ALU.add)
            nc.vector.tensor_tensor(S[:, DX:].rearrange("p (a b) -> p a b", b=HF), w1[:, 0:HF, HF:],
                                    w1[:, HF:, 0:HF].rearrange("p b a -> p a b"), ALU.add).then_inc(chain, 1)
            links[0] += 1
            dve.wait_ge(chain, links[0])
            SX = S[:, DX:].rearrange("p (a b) -> p b a", b=HF)
            full = HF // GA
            rest = HF - full * GA
            j2 = (full + 1) * GA - HF
            nc.vector.tensor_copy(SG[:, 0:full, 0:GA, :], w1[:, 0:full * GA, 0:HF].rearrange(
                "p (s q) i -> p s q i", q=GA))
            nc.vector.tensor_copy(SG[:, full, 0:rest, :], w1[:, full * GA:HF, 0:HF])
            nc.vector.tensor_copy(SG[:, full, rest:GA, :], SX[:, 0:j2, :])
            for s in range(full + 1, JG):
                j = s * GA - HF
                nc.vector.tensor_copy(SG[:, s, 0:GA, :], SX[:, j:j + GA, :])
            nc.vector.tensor_copy(SG[:, JG - 1, GA + 1, :], SX[:, HF - 1, :])
            nc.vector.tensor_copy(SG[:, 0:JG - 1, GA:GBLK, :], w1[:, HF:F - 1, HF:].rearrange(
                "p (s q) i -> p s q i", q=GB))
            nc.vector.tensor_copy(SG[:, JG - 1, GA, :], w1[:, F - 1, HF:]).then_inc(sg_ready, 1)
            dve.wait_ge(b1_in, 16)
            link(nc.vector.tensor_copy(SR[0][:, :], S[:, :]))
            nc.vector.tensor_tensor(SR[1][:, :], S[:, :], SR[0][:, :].bitcast(fp32), ALU.subtract).then_inc(s_ready, 1)
            for n in range(W2T_AT, N_W2T):
                j = prep[n][1]
                m = min(W_AT_ONCE, F - j)
                dve.wait_ge(prep_sb, n + 1)
                nc.vector.tensor_tensor(w2T[1][:, j:j + m, :], prep_bank(n)[:, 0:m * P].rearrange(
                    "p (j h) -> p j h", h=H), w2T[0][:, j:j + m, :].bitcast(fp32), ALU.subtract).then_inc(low_ok, 1)
            dve.wait_ge(b12_in, 32)
            nc.vector.tensor_scalar(b12k[:, :], b12[:, :], float(K), None, ALU.mult).then_inc(b12k_ok, 1)

            def side(t, lo):
                half = int(lo >= HF)
                base = half * PB
                return PT[:, base + (EA, EB)[half]:base + (EA, EB)[half] + HF, :], base, half

            def fields(t, p):
                lo, hi = PARTS[p:p + 2]
                e, base, half = side(t, lo)
                a, b = lo - half * HF, hi - half * HF
                dve.wait_ge(gathered[t][p], 16 * (hi - lo))
                if t and p < 2:
                    dve.wait_ge(c_ps, UNITS * (t - 1) + NB * (half + 1))
                nc.vector.transpose(e[:, a:b, :].rearrange("p f g -> p (f g)"),
                                    E[:, t, lo:hi, :].rearrange("p f k -> p (f k)")).then_inc(e_ok, 1)
                if t == 0 or hi == F:
                    dve.wait_ge(e_ok, t * NPART + p + 1)
                    for q in range(Q):
                        rows = slice(q * K, (q + 1) * K)
                        last = nc.vector.tensor_copy(BD[t % 2][rows, :, q * F + lo:q * F + hi],
                                                     e[rows, a:b, :].rearrange("p f g -> p g f"))
                    if hi == F:
                        last.then_inc(bd_last, 1)

            def products(t, p, end):
                lo, hi = PARTS[p], PARTS[end]
                e, base, half = side(t, lo)
                a, b = lo - half * HF, hi - half * HF
                dve.wait_ge(e_ok, t * NPART + end)
                sq = base + SQ[half]
                last = nc.vector.tensor_tensor(PT[:, sq + a:sq + b, :], e[:, a:b, :], e[:, a:b, :], ALU.mult)
                for n in range(max(a, 1), b):
                    last = nc.vector.tensor_tensor(PT[:, base + off(n):base + off(n) + n, :], e[:, 0:n, :],
                                                   e[:, n:n + 1, :].to_broadcast([P, n, NG]), ALU.mult)
                last.then_inc(pair_ok, 1)

            def pairs(t):
                fields(t, 0)
                if t == 1:
                    fields(t, 1)
                products(t, 0, 1)
                if t != 1:
                    fields(t, 1)
                    products(t, 1, 2)
                    if t:
                        l1_out(t - 1)
                fields(t, 2)
                if t == 1:
                    products(t, 1, 2)
                fields(t, 3)
                if t == 1:
                    l1_out(0)
                products(t, 2, 4)

            def l1_sum_part(t, c):
                dve.wait_ge(l1_ps, C1 * t + c + 1)
                nc.vector.tensor_tensor(h1[:, c, :], bank[c][:, 0:P], hd[:, c, t, :], ALU.add).then_inc(l1_sum, 1)

            def l1_clip_part(t, c):
                dve.wait_ge(l1_sum, C1 * t + c + 1)
                nc.vector.tensor_scalar(h1[:, c, :], h1[:, c, :], 0.0, None, ALU.max).then_inc(l1_ok, 1)

            def l1_out(t):
                l1_sum_part(t, 0)
                l1_clip_part(t, 0)
                l1_sum_part(t, 1)
                for c in range(2, C1):
                    l1_sum_part(t, c)
                    l1_clip_part(t, c - 1)
                l1_clip_part(t, C1 - 1)

            Df = D[:, :, :].rearrange("p j n -> p (j n)")

            def add_cross():
                dve.wait_ge(prep_sb, len(prep))
                X = D[:, :, DX:].rearrange("p j (a b) -> p j a b", b=HF)
                sa, sb_ = SQ[0], DB + SQ[1]
                last = None
                a, b = D[:, HF:, sa:sa + HF], D[:, 0:HF, sb_:sb_ + HF]
                xa = Df[:, DX:DX + HF * (ND + HF)].rearrange("p (n w) -> p n w", w=ND + HF)[:, :, 0:HF]
                at = HF * ND + DX
                xb = late[:, at:at + HF * (ND + 1)].rearrange("p (n w) -> p n w", w=ND + 1)[:, :, 0:HF * HF:HF]
                nc.vector.tensor_tensor(a, a, xa.rearrange("p n b -> p b n"), ALU.add)
                nc.vector.tensor_tensor(b, b, xb.rearrange("p n a -> p a n"), ALU.add)
                for order in range(2):
                    for n in range(1, HF):
                        a = D[:, HF:, off(n):off(n) + n]
                        b = D[:, 0:HF, DB + off(n):DB + off(n) + n]
                        xa, xb = ((X[:, 0:n, n, :].rearrange("p x b -> p b x"),
                                   X[:, HF:HF + n, :, n].rearrange("p x a -> p a x")),
                                  (X[:, n, 0:n, :].rearrange("p x b -> p b x"), X[:, HF + n, :, 0:n]))[order]
                        nc.vector.tensor_tensor(a, a, xa, ALU.add)
                        last = nc.vector.tensor_tensor(b, b, xb, ALU.add)
                    if order == 0:
                        link(last)
                last.then_inc(cross_ok, 1)

            def inner():
                for h, (j0, base) in enumerate(((0, 0), (HF, DB))):
                    vp, sq = VP[h], SQ[h]
                    vf = vp.rearrange("p j n -> p (j n)")
                    for n in range(1, HF):
                        run_n = D[:, j0:j0 + n, base + off(n):base + off(n) + n]
                        last = nc.vector.tensor_tensor(PS[:, n, 0:n, 0:n], run_n, run_n.rearrange("p y x -> p x y"),
                                                       ALU.add)
                        nc.vector.tensor_tensor(vp[:, n, off(n):off(n) + n],
                                                D[:, j0 + n, base + off(n):base + off(n) + n],
                                                D[:, j0:j0 + n, base + sq + n], ALU.add)
                        first = j0 * ND + base + off(n)
                        nc.vector.tensor_tensor(vp[:, n, sq:sq + n], D[:, j0 + n, base + sq:base + sq + n],
                                                Df[:, first:first + (n - 1) * (ND + 1) + 1:ND + 1], ALU.add)
                    link(last)
                    for n in range(1, HF - 1):
                        nc.vector.tensor_tensor(vp[:, n + 1:, off(n):off(n) + n],
                                                D[:, j0 + n + 1:j0 + HF, base + off(n):base + off(n) + n],
                                                PS[:, n + 1:, n, 0:n], ALU.add)
                    first = j0 * ND + base + sq
                    last = nc.vector.tensor_copy(vf[:, sq::TALL[h] + 1][:, 0:HF],
                                                 Df[:, first:first + (HF - 1) * (ND + 1) + 1:ND + 1])
                    if h == 0:
                        last = nc.vector.tensor_copy(vp[:, :, ONE], D[:, 0:HF, ONE])
                    link(last)
                    for n in range(HF - MC):
                        r0, k = run(n, h)
                        to, r1 = moved_to(n, h)
                        last = nc.vector.tensor_copy(vp[:, to, r1:r1 + k], vp[:, n, r0:r0 + k])
                last.then_inc(inner_ok, 1)

            dve.wait_ge(prep_ps, N_W2T)
            for vp in VP:
                link(nc.vector.memset(vp[:, HF - MC:, :], 0.0))
            pairs(0)
            add_cross()
            inner()
            pairs(1)
            for t in range(2, T):
                pairs(t)
            l1_out(T - 1)

        @block.scalar
        def _(act):
            act.dma_start(wt1d[:, :], x["W_top1"][2 * P:, :]).then_inc(wt1d_in, 16)
            act.dma_start(bt1[:, :], x["b_top1"].rearrange("(p c) -> p c", c=C1)).then_inc(bt1_in, 16)

            def empty(plan, first):
                for n, (kind, j) in enumerate(plan, first):
                    act.wait_ge(prep_ps, n + 1)
                    src = prep_bank(n)
                    if kind == "d":
                        dst, src = dT[:, :], src[0:DC, 0:T * P]
                    elif kind == "D":
                        dst, src = D[:, j, :], src[:, 0:ND]
                    elif kind == "hd":
                        pass
                    elif kind == "w1":
                        m, rows = w1_slots(j), g_rows(j)
                        dst, src = W1G[0:rows, j:j + m, :], src[0:rows, 0:m * P].rearrange("p (j h) -> p j h", h=H)
                    else:
                        m = min(W_AT_ONCE, F - j)
                        dst, src = w2T[0][:, j:j + m, :], src[:, 0:m * P].rearrange("p (j h) -> p j h", h=H)
                    if kind == "hd":
                        if j == 0:
                            act.wait_ge(bt1_in, 16)
                        nc.scalar.activation(hd[:, j, :, :].rearrange("p t b -> p (t b)"), src[:, 0:T * P],
                                             ACT.Identity, bias=bt1[:, j:j + 1]).then_inc(prep_sb, 1)
                    else:
                        nc.scalar.copy(dst, src).then_inc(prep_sb, 1)

            def empty_late(plan, first):
                for n, (h, c) in enumerate(plan, first):
                    act.wait_ge(prep_ps, n + 1)
                    m, rows = late_cols(c), late_rows(h, c)
                    nc.scalar.copy(V[h][0:rows, c:c + m, :], prep_bank(n)[0:rows, 0:m * P].rearrange(
                        "p (j h) -> p j h", h=H)).then_inc(prep_sb, 1)

            def block_diagonal(t, first=0, end=NPART - 1):
                if t == 1:
                    act.wait_ge(bd_zero, 2)
                if t >= 2:
                    act.wait_ge(c_ps, UNITS * (t - 1))
                for p in range(first, end):
                    act.wait_ge(e_ok, NPART * t + p + 1)
                    half = int(PARTS[p] >= HF)
                    e, c = (EA, PB + EB)[half], half * HF
                    lo, hi = PARTS[p] - c, PARTS[p + 1] - c
                    for q in range(Q):
                        rows = slice(q * K, (q + 1) * K)
                        last = nc.scalar.copy(BD[t % 2][rows, :, q * F + c + lo:q * F + c + hi],
                                              PT[rows, e + lo:e + hi, :].rearrange("p f g -> p g f"))
                if end == NPART - 1:
                    last.then_inc(bd_ok, 1)

            def moments(t, first=0, end=UNITS):
                if t >= 2:
                    act.wait_ge(f_done, t - 1)
                for n in range(first, end):
                    u = UNITS * t + n
                    act.wait_ge(c_ps, u + 1)
                    C, rows = ((CA, MA), (CB, MB))[n // NB]
                    g0 = (n % NB) * GP
                    dst = C[t % 2][0:rows, :, :].rearrange("s j (q g) -> s g q j", q=Q)[:, g0:g0 + GP, :, :]
                    src = bank[u % RING][0:rows, 0:GP * Q * F].rearrange("s (g q j) -> s g q j", g=GP, q=Q)
                    nc.scalar.copy(dst, src).then_inc(c_sb, 1)

            def z_out(t):
                act.wait_ge(z2_ps, t + 1)
                if t == 0:
                    act.wait_ge(b12k_ok, 1)
                nc.scalar.activation(z[:, 1, :], bank[4][:, 0:P], ACT.Identity, bias=b12k[:, 1:2]).then_inc(z2_ok, 1)
                act.wait_ge(f_done, t + 1)
                nc.scalar.activation(z[:, 0, :], bank[5][:, 0:P], ACT.Identity, bias=b12k[:, 0:1]).then_inc(z1_ok, 1)

            def l2_out(t):
                if t == 0:
                    act.wait_ge(top_in, 16 * 4)
                for c in range(C2):
                    act.wait_ge(l2_ps, C2 * t + c + 1)
                    nc.scalar.activation(h2[:, c, :], bank[L2_BANK[c]][:, 0:P], ACT.Relu,
                                         bias=bt2[:, c:c + 1]).then_inc(l2_ok, 1)

            def l3_out(t):
                act.wait_ge(l3_ps, t + 1)
                nc.scalar.copy(y[:, t, :], bank[L2_BANK[0]][0:1, 2 * P:3 * P]).then_inc(y_ok, 1)

            empty(prep, 0)
            moments(0, 0, CUT)
            empty_late(late_cross, len(prep))
            moments(0, CUT)
            empty_late(late_inner, N_CROSS)
            for t in range(1, T):
                block_diagonal(t, 0, 2)
                z_out(t - 1)
                block_diagonal(t, 2)
                if t >= DENSE_FIRST:
                    l2_out(t - 1)
                    moments(t, 0, AT_L3)
                    l3_out(t - 1)
                    moments(t, AT_L3)
                else:
                    moments(t)
                    l2_out(t - 1)
                    l3_out(t - 1)
            z_out(T - 1)
            l2_out(T - 1)
            l3_out(T - 1)

        @block.tensor
        def _(pe):
            def fill(plan, first):
                for n, (kind, j) in enumerate(plan, first):
                    if n >= RING:
                        pe.wait_ge(prep_sb, n - RING + 1)
                        if plan[n - RING][0] == "w2T":
                            pe.wait_ge(low_ok, n - RING - W2T_AT + 1)
                    ps = prep_bank(n)
                    if kind == "w2T":
                        pe.wait_ge(w2_in, 16)
                        for i in range(j, min(j + W_AT_ONCE, F)):
                            last = nc.tensor.transpose(ps[:, (i - j) * P:(i - j + 1) * P], w2[:, :, i], ident[:, :])
                    elif kind == "d":
                        pe.wait_ge(dn_in, 16)
                        for t in range(T):
                            last = nc.tensor.transpose(ps[0:DC, t * P:(t + 1) * P], dn[:, t, :], ident[:, :])
                    elif kind == "hd":
                        if j == 0:
                            pe.wait_ge(prep_sb, 1)
                            pe.wait_ge(wt1d_in, 16)
                        last = nc.tensor.matmul(ps[:, 0:T * P], wt1d[:, j::C1], dT[:, :], start=True, stop=True)
                    elif kind == "D":
                        if j == 0:
                            pe.wait_ge(prep_sb, N_W2T)
                            pe.wait_ge(low_ok, N_W2T - W2T_AT)
                            pe.wait_ge(s_ready, 1)
                        for n_, (a, b) in enumerate(((0, 0), (0, 1), (1, 0))):
                            last = nc.tensor.matmul(ps[:, 0:ND], w2T[a][:, j, :], SR[b][:, :], start=(n_ == 0),
                                                    stop=(n_ == 2))
                    elif kind == "w1":
                        pe.wait_ge(sg_ready, 1)
                        for s in range(j, j + w1_slots(j)):
                            k = g_rows(s)
                            src = SG[:, s, :, :].rearrange("m q i -> m (q i)")[:, 0:k]
                            last = nc.tensor.transpose(ps[0:k, (s - j) * P:(s - j + 1) * P], src, ident[:, :])
                    last.then_inc(prep_ps, 1)

            def fill_late(plan, first):
                for n, (h, c) in enumerate(plan, first):
                    pe.wait_ge(prep_sb, min(n - RING + 1, N_CROSS))
                    rows = late_rows(h, c)
                    for i in range(late_cols(c)):
                        if c < HF:
                            src = D[:, (1 - h) * HF + c + i, h * DB:h * DB + rows]
                        else:
                            src = VP[h][:, c + i - HF + HF - MC, 0:rows]
                        last = nc.tensor.transpose(prep_bank(n)[0:rows, i * P:(i + 1) * P], src, ident[:, :])
                    last.then_inc(prep_ps, 1)

            def moments(t, first=0, end=UNITS):
                if first == 0 and end:
                    pe.wait_ge(pair_ok, PAIRS * t + 1)
                    pe.wait_ge(bd_last, t + 1)
                    if t:
                        pe.wait_ge(bd_ok, t)
                for n in range(first, end):
                    u = UNITS * t + n
                    if n == NB:
                        pe.wait_ge(pair_ok, PAIRS * (t + 1))
                    if u >= RING:
                        pe.wait_ge(c_sb, u - RING + 1)
                    if t and n < min(C1, RING):
                        pe.wait_ge(l1_sum, C1 * (t - 1) + n + 1)
                    lo, m = ((0, MA), (PB, MB))[n // NB]
                    for i in range(GP):
                        g = (n % NB) * GP + i
                        last = nc.tensor.matmul(bank[u % RING][0:m, i * Q * F:(i + 1) * Q * F],
                                                PT[:, lo:lo + m, g], BD[t % 2][:, g, :], start=True, stop=True)
                    last.then_inc(c_ps, 1)

            def final_cross(t, h):
                pe.wait_ge(c_sb, UNITS * t + NB * (h + 1))
                if h == 0 and t == 0:
                    pe.wait_ge(prep_sb, N_CROSS)
                for j in range(HF):
                    nc.tensor.matmul(bank[4][:, 0:P], V[h][0:ROWS[h], j, :],
                                     (CA, CB)[h][t % 2][0:ROWS[h], (1 - h) * HF + j, :],
                                     start=(h == 0 and j == 0), stop=False)

            def final_inner(t, h):
                pe.wait_ge(m_in[h][t % 2], 16 * len(MOVES) * (t // 2 + 1))
                if t == 0:
                    pe.wait_ge(prep_sb, N_ALL if h else N_CROSS + len(late_inner) // 2)
                for j in range(MC):
                    last = nc.tensor.matmul(bank[4][:, 0:P], V[h][0:TALL[h], HF + j, :],
                                            (CA, CB)[h][t % 2][0:TALL[h], h * HF + HF - MC + j, :],
                                            start=False, stop=(h == 1 and j == MC - 1))
                if h == 1:
                    last.then_inc(z2_ps, 1)

            def final_g(t):
                by_pool = len(G_LATE) * (t == T - 1)
                if by_pool:
                    pe.wait_ge(g_in_pool, 16 * by_pool)
                pe.wait_ge(g_in[t % 2], 16 * (G_MOVES * (t // 2 + 1) - by_pool))
                for s in range(JG):
                    k = g_rows(s)
                    last = nc.tensor.matmul(bank[5][:, 0:P], W1G[0:k, s, :], G4[t % 2][0:k, s, :],
                                            start=(s == 0), stop=(s == JG - 1))
                last.then_inc(f_done, 1)

            def layer1(t):
                if t == 0:
                    pe.wait_ge(top_in, 16 * 4)
                pe.wait_ge(z2_ok, t + 1)
                for c in range(C1):
                    nc.tensor.matmul(bank[c][:, 0:P], wt1[:, 1, c::C1], z[:, 1, :], start=True, stop=False)
                pe.wait_ge(z1_ok, t + 1)
                for c in range(C1):
                    nc.tensor.matmul(bank[c][:, 0:P], wt1[:, 0, c::C1], z[:, 0, :], start=False,
                                     stop=True).then_inc(l1_ps, 1)

            def layer2(t):
                if t >= 1:
                    pe.wait_ge(y_ok, t)
                for i in range(C1):
                    pe.wait_ge(l1_ok, C1 * t + i + 1)
                    for c in range(C2):
                        last = nc.tensor.matmul(bank[L2_BANK[c]][:, 0:P], wt2[:, i, c::C2], h1[:, i, :],
                                                start=(i == 0), stop=(i == C1 - 1))
                        if i == C1 - 1:
                            last.then_inc(l2_ps, 1)

            def layer3(t):
                for i in range(C2):
                    pe.wait_ge(l2_ok, C2 * t + i + 1)
                    last = nc.tensor.matmul(bank[L2_BANK[0]][0:1, 2 * P:3 * P], wt3[:, i:i + 1], h2[:, i, :],
                                            start=(i == 0), stop=(i == C2 - 1))
                last.then_inc(l3_ps, 1)

            pe.wait_ge(ident_ok, 1)
            fill(prep, 0)
            moments(0, 0, CUT)
            pe.wait_ge(cross_ok, 1)
            fill_late(late_cross, len(prep))
            moments(0, CUT)
            final_cross(0, 0)
            final_cross(0, 1)
            pe.wait_ge(inner_ok, 1)
            fill_late(late_inner, N_CROSS)
            final_inner(0, 0)
            final_inner(0, 1)
            final_g(0)
            for t in range(1, T):
                layer1(t - 1)
                if t >= DENSE_FIRST:
                    layer2(t - 1)
                    layer3(t - 1)
                    moments(t)
                    final_cross(t, 0)
                else:
                    moments(t, 0, AT_L2)
                    layer2(t - 1)
                    moments(t, AT_L2)
                    final_cross(t, 0)
                    layer3(t - 1)
                final_cross(t, 1)
                final_inner(t, 0)
                final_inner(t, 1)
                final_g(t)
            layer1(T - 1)
            layer2(T - 1)
            layer3(T - 1)


def kernel(**inputs):
    import numpy as _np
    import concourse.bacc as _bacc
    from concourse import mybir as _mybir
    from concourse.bass_utils import run_bass_kernel_spmd as _run

    nc = _bacc.Bacc("TRN2", target_bir_lowering=False, num_devices=1)
    arrays, args = {}, {}
    for name in inputs:
        a = _np.ascontiguousarray(inputs[name])
        arrays[f"in_{name}_dram"] = a
        args[name] = nc.dram_tensor(f"in_{name}_dram", a.shape, _mybir.dt.from_np(a.dtype), kind="ExternalInput").ap()
    rows = inputs["ids"].shape[0]
    out = nc.dram_tensor("out_0_dram", (rows, 1), _mybir.dt.float32, kind="ExternalOutput").ap()
    dlrm_cin_tower(nc, args, out)
    r = _run(nc, [arrays], core_ids=[0])
    return r.results[0]["out_0_dram"]
```
